# Optimizing a Trainium2 kernel written in Bass

```python
import numpy as np
import jax
import jax.numpy as jnp

def _softmax(x, axis=-1):
    return jax.nn.softmax(x, axis=axis)

def _gelu(x):
    return jax.nn.gelu(x, approximate=True)

def _silu(x):
    return jax.nn.silu(x)

def _sigmoid(x):
    return jax.nn.sigmoid(x)

def _layernorm(x, axis=-1, eps=1e-05):
    m = jnp.mean(x, axis=axis, keepdims=True)
    v = jnp.var(x, axis=axis, keepdims=True)
    return (x - m) / jnp.sqrt(v + eps)

def _scatter_add(tgt, idx, src, axis=0):
    return tgt.at[idx].add(src)

def _segment_sum(src, seg, n):
    return jax.ops.segment_sum(src, seg, n)
kernel_name = 'mk_seq_preln_d1_jaxref_r8_75443b'

def setup_inputs(seed: int=0):
    np.random.seed(seed)
    _w = jnp.asarray

    def _L0_attn_setup():
        import jax, jax.numpy as jnp
        from jax import lax
        import numpy as np
        D_MODEL = 128
        D_STATE = 16
        D_CONV = 4
        EXPAND = 2
        D_INNER = EXPAND * D_MODEL
        DT_RANK = D_MODEL // 16
        EPS = 1e-05

        def _ln(x, g, b):
            mu = jnp.mean(x, axis=-1, keepdims=True)
            var = jnp.mean(jnp.square(x - mu), axis=-1, keepdims=True)
            return (x - mu) * lax.rsqrt(var + EPS) * g + b

        def _mamba(u, in_proj_w, conv_w, conv_b, x_proj_w, dt_w, dt_b, A_log, D, out_w):
            Bsz, L, _ = u.shape
            xz = u @ in_proj_w.T
            x_in, z = jnp.split(xz, 2, axis=-1)
            xc = x_in.transpose(0, 2, 1)
            xc = lax.conv_general_dilated(xc, conv_w, window_strides=(1,), padding=[(D_CONV - 1, 0)], dimension_numbers=('NCH', 'OIH', 'NCH'), feature_group_count=D_INNER)
            xc = jax.nn.silu(xc + conv_b[None, :, None]).transpose(0, 2, 1)
            x_dbl = xc @ x_proj_w.T
            dt, Bm, Cm = jnp.split(x_dbl, [DT_RANK, DT_RANK + D_STATE], axis=-1)
            delta = jax.nn.softplus(dt @ dt_w.T + dt_b)
            A = -jnp.exp(A_log)
            dA = jnp.exp(jnp.einsum('bld,dn->bldn', delta, A))
            dBu = jnp.einsum('bld,bln,bld->bldn', delta, Bm, xc)

            def step(h, inp):
                dA_t, dBu_t, C_t = inp
                h = dA_t * h + dBu_t
                y = jnp.einsum('bdn,bn->bd', h, C_t)
                return (h, y)
            h0 = jnp.zeros((Bsz, D_INNER, D_STATE), u.dtype)
            _, ys = lax.scan(step, h0, (dA.transpose(1, 0, 2, 3), dBu.transpose(1, 0, 2, 3), Cm.transpose(1, 0, 2)))
            y = ys.transpose(1, 0, 2) + xc * D
            y = y * jax.nn.silu(z)
            return y @ out_w.T
        key = jax.random.key(seed)
        ks = jax.random.split(key, 16)
        B, L = (2, 128)
        s = 0.02
        inp = {'x': jax.random.normal(ks[0], (B, L, D_MODEL), jnp.float32), 'n1_g': jnp.ones((D_MODEL,), jnp.float32), 'n1_b': jnp.zeros((D_MODEL,), jnp.float32), 'n2_g': jnp.ones((D_MODEL,), jnp.float32), 'n2_b': jnp.zeros((D_MODEL,), jnp.float32), 'in_proj_w': jax.random.normal(ks[1], (2 * D_INNER, D_MODEL), jnp.float32) * s, 'conv_w': jax.random.normal(ks[2], (D_INNER, 1, D_CONV), jnp.float32) * 0.1, 'conv_b': jnp.zeros((D_INNER,), jnp.float32), 'x_proj_w': jax.random.normal(ks[3], (DT_RANK + 2 * D_STATE, D_INNER), jnp.float32) * s, 'dt_w': jax.random.normal(ks[4], (D_INNER, DT_RANK), jnp.float32) * s, 'dt_b': jnp.full((D_INNER,), -4.0, jnp.float32) + jax.random.normal(ks[5], (D_INNER,), jnp.float32) * 0.1, 'A_log': jnp.tile(jnp.log(jnp.arange(1, D_STATE + 1, dtype=jnp.float32))[None, :], (D_INNER, 1)), 'D': jnp.ones((D_INNER,), jnp.float32), 'out_w': jax.random.normal(ks[6], (D_MODEL, D_INNER), jnp.float32) * s, 'ffg_w': jax.random.normal(ks[7], (2 * D_MODEL, D_MODEL), jnp.float32) * s, 'ffg_b': jnp.zeros((2 * D_MODEL,), jnp.float32), 'ffp_w': jax.random.normal(ks[8], (D_MODEL, D_MODEL), jnp.float32) * s, 'ffp_b': jnp.zeros((D_MODEL,), jnp.float32)}
        return inp
    _L0_attn_in = _L0_attn_setup()

    def _L0_ffn_setup():
        import jax, jax.numpy as jnp
        import numpy as np
        D, F, E, K = (128, 344, 8, 2)
        key = jax.random.key(seed)
        k0, k1, k2, k3, k4 = jax.random.split(key, 5)
        s = 0.02
        x = jax.random.normal(k0, (2, 64, D), jnp.float32)
        Ws = jax.random.normal(k1, (D, E), jnp.float32) * s
        bs = jnp.zeros((E,), jnp.float32)
        Wg = jax.random.normal(k2, (E, D, F), jnp.float32) * s
        Wu = jax.random.normal(k3, (E, D, F), jnp.float32) * s
        Wd = jax.random.normal(k4, (E, F, D), jnp.float32) * s
        return {'x': x, 'Ws': Ws, 'bs': bs, 'Wg': Wg, 'Wu': Wu, 'Wd': Wd}
    _L0_ffn_in = _L0_ffn_setup()
    _d = {'L0_attn_x': _L0_attn_in['x'], 'L0_attn_n1_g': _L0_attn_in['n1_g'], 'L0_attn_n1_b': _L0_attn_in['n1_b'], 'L0_attn_n2_g': _L0_attn_in['n2_g'], 'L0_attn_n2_b': _L0_attn_in['n2_b'], 'L0_attn_in_proj_w': _L0_attn_in['in_proj_w'], 'L0_attn_conv_w': _L0_attn_in['conv_w'], 'L0_attn_conv_b': _L0_attn_in['conv_b'], 'L0_attn_x_proj_w': _L0_attn_in['x_proj_w'], 'L0_attn_dt_w': _L0_attn_in['dt_w'], 'L0_attn_dt_b': _L0_attn_in['dt_b'], 'L0_attn_A_log': _L0_attn_in['A_log'], 'L0_attn_D': _L0_attn_in['D'], 'L0_attn_out_w': _L0_attn_in['out_w'], 'L0_attn_ffg_w': _L0_attn_in['ffg_w'], 'L0_attn_ffg_b': _L0_attn_in['ffg_b'], 'L0_attn_ffp_w': _L0_attn_in['ffp_w'], 'L0_attn_ffp_b': _L0_attn_in['ffp_b'], 'L0_ffn_Ws': _L0_ffn_in['Ws'], 'L0_ffn_bs': _L0_ffn_in['bs'], 'L0_ffn_Wg': _L0_ffn_in['Wg'], 'L0_ffn_Wu': _L0_ffn_in['Wu'], 'L0_ffn_Wd': _L0_ffn_in['Wd']}
    _x0 = _d['L0_attn_x']
    _d['L0_attn_x'] = jax.random.normal(jax.random.fold_in(jax.random.key(seed), 1), (2, 2048, 128), dtype=_x0.dtype)
    del _x0
    return _d

def reference(L0_attn_x, L0_attn_n1_g, L0_attn_n1_b, L0_attn_n2_g, L0_attn_n2_b, L0_attn_in_proj_w, L0_attn_conv_w, L0_attn_conv_b, L0_attn_x_proj_w, L0_attn_dt_w, L0_attn_dt_b, L0_attn_A_log, L0_attn_D, L0_attn_out_w, L0_attn_ffg_w, L0_attn_ffg_b, L0_attn_ffp_w, L0_attn_ffp_b, L0_ffn_Ws, L0_ffn_bs, L0_ffn_Wg, L0_ffn_Wu, L0_ffn_Wd):

    def _L0_attn_ref(x, n1_g, n1_b, n2_g, n2_b, in_proj_w, conv_w, conv_b, x_proj_w, dt_w, dt_b, A_log, D, out_w, ffg_w, ffg_b, ffp_w, ffp_b):
        import jax, jax.numpy as jnp
        from jax import lax
        import numpy as np
        D_MODEL = 128
        D_STATE = 16
        D_CONV = 4
        EXPAND = 2
        D_INNER = EXPAND * D_MODEL
        DT_RANK = D_MODEL // 16
        EPS = 1e-05

        def _ln(x, g, b):
            mu = jnp.mean(x, axis=-1, keepdims=True)
            var = jnp.mean(jnp.square(x - mu), axis=-1, keepdims=True)
            return (x - mu) * lax.rsqrt(var + EPS) * g + b

        def _mamba(u, in_proj_w, conv_w, conv_b, x_proj_w, dt_w, dt_b, A_log, D, out_w):
            Bsz, L, _ = u.shape
            xz = u @ in_proj_w.T
            x_in, z = jnp.split(xz, 2, axis=-1)
            xc = x_in.transpose(0, 2, 1)
            xc = lax.conv_general_dilated(xc, conv_w, window_strides=(1,), padding=[(D_CONV - 1, 0)], dimension_numbers=('NCH', 'OIH', 'NCH'), feature_group_count=D_INNER)
            xc = jax.nn.silu(xc + conv_b[None, :, None]).transpose(0, 2, 1)
            x_dbl = xc @ x_proj_w.T
            dt, Bm, Cm = jnp.split(x_dbl, [DT_RANK, DT_RANK + D_STATE], axis=-1)
            delta = jax.nn.softplus(dt @ dt_w.T + dt_b)
            A = -jnp.exp(A_log)
            dA = jnp.exp(jnp.einsum('bld,dn->bldn', delta, A))
            dBu = jnp.einsum('bld,bln,bld->bldn', delta, Bm, xc)

            def step(h, inp):
                dA_t, dBu_t, C_t = inp
                h = dA_t * h + dBu_t
                y = jnp.einsum('bdn,bn->bd', h, C_t)
                return (h, y)
            h0 = jnp.zeros((Bsz, D_INNER, D_STATE), u.dtype)
            _, ys = lax.scan(step, h0, (dA.transpose(1, 0, 2, 3), dBu.transpose(1, 0, 2, 3), Cm.transpose(1, 0, 2)))
            y = ys.transpose(1, 0, 2) + xc * D
            y = y * jax.nn.silu(z)
            return y @ out_w.T
        x = x + _mamba(_ln(x, n1_g, n1_b), in_proj_w, conv_w, conv_b, x_proj_w, dt_w, dt_b, A_log, D, out_w)
        normed = _ln(x, n2_g, n2_b)
        gate, val = jnp.split(normed @ ffg_w.T + ffg_b, 2, axis=-1)
        x = x + jax.nn.silu(gate) * val @ ffp_w.T + ffp_b
        return x

    def _L0_ffn_ref(x, Ws, bs, Wg, Wu, Wd):
        import jax, jax.numpy as jnp
        import numpy as np
        D, F, E, K = (128, 344, 8, 2)
        b, n, d = x.shape
        xt = x.reshape(-1, d)
        logits = xt @ Ws + bs
        topk_w, topk_idx = jax.lax.top_k(logits, K)
        topk_w = jax.nn.softmax(topk_w, axis=-1)
        combine = jnp.sum(jax.nn.one_hot(topk_idx, E, dtype=xt.dtype) * topk_w[..., None], axis=1)
        g = jnp.einsum('td,edf->tef', xt, Wg)
        u = jnp.einsum('td,edf->tef', xt, Wu)
        h = jax.nn.silu(g) * u
        y = jnp.einsum('tef,efd->ted', h, Wd)
        out = jnp.einsum('ted,te->td', y, combine)
        return out.reshape(b, n, d)
    x = L0_attn_x
    x = x + _L0_attn_ref(_layernorm(x, axis=-1), L0_attn_n1_g, L0_attn_n1_b, L0_attn_n2_g, L0_attn_n2_b, L0_attn_in_proj_w, L0_attn_conv_w, L0_attn_conv_b, L0_attn_x_proj_w, L0_attn_dt_w, L0_attn_dt_b, L0_attn_A_log, L0_attn_D, L0_attn_out_w, L0_attn_ffg_w, L0_attn_ffg_b, L0_attn_ffp_w, L0_attn_ffp_b)
    x = x + _L0_ffn_ref(_layernorm(x, axis=-1), L0_ffn_Ws, L0_ffn_bs, L0_ffn_Wg, L0_ffn_Wu, L0_ffn_Wd)
    return x

_drawn_inputs = setup_inputs


def setup_inputs(seed=0):
    import zlib

    import numpy as np

    out = dict(_drawn_inputs(seed))
    spreads = {'L0_attn_n1_g': (1.0, 0.6),
     'L0_attn_n1_b': (0.0, 0.8),
     'L0_attn_n2_g': (1.0, 0.6),
     'L0_attn_n2_b': (0.0, 0.8),
     'L0_attn_conv_b': (0.0, 0.8),
     'L0_attn_D': (1.0, 0.6),
     'L0_attn_ffg_b': (0.0, 0.8),
     'L0_attn_ffp_b': (0.0, 0.1),
     'L0_ffn_bs': (0.0, 0.8)}
    factors = {'L0_attn_in_proj_w': 8.0,
     'L0_attn_conv_w': 8.0,
     'L0_attn_x_proj_w': 8.0,
     'L0_attn_dt_w': 8.0,
     'L0_attn_dt_b': 8.0,
     'L0_attn_A_log': 8.0,
     'L0_attn_out_w': 8.0,
     'L0_attn_ffg_w': 8.0,
     'L0_attn_ffp_w': 8.0,
     'L0_ffn_Ws': 8.0,
     'L0_ffn_Wg': 8.0,
     'L0_ffn_Wu': 8.0,
     'L0_ffn_Wd': 8.0}
    for name, (base, spread) in spreads.items():
        noise = np.random.default_rng([zlib.crc32(name.encode()), seed]).standard_normal(out[name].shape)
        drawn = base * np.exp(spread * noise) if base else spread * noise
        out[name] = jnp.asarray(drawn.astype(out[name].dtype))
    for name, factor in factors.items():
        out[name] = (out[name] * factor).astype(out[name].dtype)
    return out
```

```python
from contextlib import ExitStack

import numpy as np

import concourse.bass as bass
from concourse import mybir

BATCH, SEQ, D_MODEL = 2, 2048, 128
TOKENS = BATCH * SEQ
D_INNER, D_STATE, D_CONV, DT_RANK = 256, 16, 4, 8
HALVES = D_INNER // 128
EXPERTS, FF = 8, 344
EPS = 1e-5
P = 128
CHUNK = 512
SUB = CHUNK // P
CHUNKS = TOKENS // CHUNK
HALO = D_CONV - 1
BC = 2 * D_STATE
PARTS = 3
F_TILES = [(f, min(P, FF - f)) for f in range(0, FF, P)]
NF = len(F_TILES)


class Program:

    def __init__(self, nc, ctx):
        self.nc, self.ctx = nc, ctx
        self.queue = {e: [] for e in ("sync", "gpsimd", "scalar", "vector", "tensor")}
        self.sems, self.count, self.seen = {}, {}, {}

    def op(self, engine, done, build, after=()):
        step = 16 if done.startswith("dma_") else 1
        if done not in self.sems:
            self.sems[done] = self.ctx.enter_context(self.nc.semaphore(done))
            self.count[done] = 0
        waits = []
        for token in after:
            if token is None:
                continue
            name, value = token
            if self.seen.get((engine, name), 0) < value:
                self.seen[(engine, name)] = value
                waits.append((self.sems[name], value))
        self.count[done] += step
        self.queue[engine].append((waits, build, self.sems[done], step))
        return (done, self.count[done])

    def wait(self, engine, after):
        waits = [(self.sems[n], v) for n, v in after]
        self.queue[engine].append((waits, None, None, 0))

    def play(self, engine, eng):
        for waits, build, sem, step in self.queue[engine]:
            for s, v in waits:
                eng.wait_ge(s, v)
            if build is not None:
                build(eng).then_inc(sem, step)


def mamba_moe_block(nc, T, out):
    f32, bf16, u32 = mybir.dt.float32, mybir.dt.bfloat16, mybir.dt.uint32
    ALU, ACT = mybir.AluOpType, mybir.ActivationFunctionType
    ctx = ExitStack()
    with ctx:
        def sb(name, shape, dt=f32):
            return ctx.enter_context(nc.sbuf_tensor(name, shape, dt))

        def bank(name):
            return ctx.enter_context(nc.psum_tensor(name, [P, CHUNK], f32))

        pr = Program(nc, ctx)

        ident = sb("ident", [P, P])
        select_row = sb("select_row", [PARTS * BC, BC, P], bf16)
        part_mask = sb("part_mask", [PARTS * BC, 2])
        iota8 = sb("iota8", [P, EXPERTS])
        w_in = sb("w_in", [P, 2 * D_INNER])
        w_conv = sb("w_conv", [P, HALVES, D_CONV])
        b_conv = sb("b_conv", [P, HALVES])
        w_xproj = sb("w_xproj", [P, HALVES, PARTS * BC + DT_RANK])
        w_dt = sb("w_dt", [P, D_INNER])
        b_dt = sb("b_dt", [P, HALVES])
        a_neg = sb("a_neg", [P, HALVES, D_STATE])
        skip_d = sb("skip_d", [P, HALVES])
        w_out = sb("w_out", [P, HALVES, D_MODEL])
        norm_gb = sb("norm_gb", [P, 4])
        w_ffg = sb("w_ffg", [P, 2 * D_MODEL])
        b_ffg = sb("b_ffg", [P, 2])
        w_ffp = sb("w_ffp", [P, D_MODEL])
        b_ffp = sb("b_ffp", [P, D_MODEL])
        w_route = sb("w_route", [P, EXPERTS])
        b_route = sb("b_route", [P, EXPERTS])
        w_gate = sb("w_gate", [P, EXPERTS, FF])
        w_up = sb("w_up", [P, EXPERTS, FF])
        w_down = sb("w_down", [P, EXPERTS, NF, D_MODEL])

        x_tok = sb("x_tok", [P, 3, SUB, D_MODEL])
        x_one = sb("x_one", [P, 3, SUB, D_MODEL])
        u_tok = sb("u_tok", [P, SUB, D_MODEL])
        u_t = sb("u_t", [P, CHUNK])
        x_in = sb("x_in", [P, 2, HALVES, HALO + CHUNK])
        conv = sb("conv", [P, HALVES, CHUNK])
        tanh_c = sb("tanh_c", [P, HALVES, CHUNK])
        xc = sb("xc", [P, 2, HALVES, CHUNK])
        tanh_z = sb("tanh_z", [P, CHUNK])
        silu_z = sb("silu_z", [P, 2, HALVES, CHUNK])
        dt_low = sb("dt_low", [P, CHUNK])
        pre_dt = sb("pre_dt", [P, HALVES, CHUNK])
        log_dt = sb("log_dt", [P, HALVES, CHUNK])
        exp_dt, ser_dt = tanh_c, conv
        small = sb("small", [P, HALVES, CHUNK], u32)
        delta = sb("delta", [P, 2, HALVES, CHUNK])
        du = sb("du", [P, 2, HALVES, CHUNK])
        bc_part = sb("bc_part", [PARTS * BC, CHUNK], bf16)
        bc_rest = sb("bc_rest", [PARTS * BC, 2, CHUNK])
        bc_stack = sb("bc_stack", [PARTS * BC, 2, CHUNK], bf16)
        b_wide = sb("b_wide", [P, 3, CHUNK])
        inflow = sb("inflow", [P, 3, HALVES, CHUNK])
        state = sb("state", [P, 2, HALVES, CHUNK])
        carry = sb("carry", [P, D_STATE, HALVES])
        prod = sb("prod", [P, 2, HALVES, CHUNK])
        y_gated = sb("y_gated", [P, HALVES, CHUNK])
        x_two = sb("x_two", [P, SUB, D_MODEL])
        n_tok = sb("n_tok", [P, SUB, D_MODEL])
        n_t = sb("n_t", [P, CHUNK])
        tanh_g = sb("tanh_g", [P, CHUNK])
        gate_h = sb("gate_h", [P, CHUNK])
        ff_h = sb("ff_h", [P, CHUNK])
        x_four = sb("x_four", [P, 2, SUB, D_MODEL])
        m_tok = sb("m_tok", [P, SUB, D_MODEL])
        m_t = sb("m_t", [P, 2, CHUNK])
        logits = sb("logits", [P, SUB, EXPERTS])
        top8 = sb("top8", [P, SUB, 8])
        top_i = sb("top_i", [P, SUB, 8], u32)
        top_if = sb("top_if", [P, SUB, 8])
        top_w = sb("top_w", [P, 4, SUB])
        hot = sb("hot", [P, SUB, EXPERTS])
        combine = sb("combine", [P, 2, SUB, EXPERTS])
        stats = sb("stats", [P, SUB, 6])
        mean_var = sb("mean_var", [P, 4, SUB, 2])
        rstd = sb("rstd", [P, 4, SUB])
        minus_half = sb("minus_half", [P, SUB])
        tanh_m = sb("tanh_m", [P, CHUNK])
        half_m = sb("half_m", [P, CHUNK])
        h_moe = sb("h_moe", [P, NF, CHUNK])

        decay_bank = [bank("decay0"), bank("decay1")]
        b_bank, c_bank = bank("b_bank"), bank("c_bank")
        y_bank = [bank("y0"), bank("y1")]
        work_bank = [bank("work0"), bank("work1")]
        work_free = [None, None]
        turn, held = [0], set()

        def work():
            turn[0] ^= 1
            assert turn[0] not in held
            held.add(turn[0])
            return turn[0], work_free[turn[0]]

        def release(g, token):
            held.discard(g)
            work_free[g] = token
            return token

        op = pr.op

        def load(dst, src, name="dma_weights", engine="sync", after=()):
            return op(engine, name, lambda e: e.dma_start(dst, src), after)

        x_dram = T["x"].rearrange("b (c s p) d -> (b c) p s d", s=SUB, p=P)
        out_dram = out.rearrange("b (c s p) d -> (b c) p s d", s=SUB, p=P)
        x_loaded, out_sent = {}, {}

        def load_x(c, after=()):
            x_loaded[c] = load(x_tok[:, c % 3], x_dram[c], f"dma_x{c % 3}", after=after)

        load_x(0)
        load(ident[:], T["ident"])
        load(w_in[:], T["in_wT"])
        load(norm_gb[:], T["norm_gb"])
        load(w_conv[:], T["conv_w"].rearrange("(h p) o k -> p h (o k)", p=P))
        load(b_conv[:], T["conv_b"])
        load(w_xproj[:], T["xproj_wT"].rearrange("(h p) m -> p h m", p=P))
        load(w_dt[PARTS * BC:PARTS * BC + DT_RANK, :], T["dt_wT"])
        load(b_dt[:], T["dt_b"])
        load(a_neg[:], T["A_log"].rearrange("(h p) n -> p h n", p=P))
        load(skip_d[:], T["D"])
        load(part_mask[:], T["part_mask"])
        front_w = load(select_row[:], T["select_row"])
        load_x(1)
        for dst, src in ((w_out[:], T["out_wT"].rearrange("(h p) m -> p h m", p=P)), (w_ffg[:], T["ffg_wT"]),
                         (b_ffg[:], T["ffg_b"]), (w_ffp[:], T["ffp_wT"]),
                         (b_ffp[:], T["ffp_b"].rearrange("(o d) -> o d", o=1).to_broadcast([P, D_MODEL])),
                         (w_route[:], T["Ws"]), (iota8[:], T["iota8"]),
                         (b_route[:], T["bs"].rearrange("(o d) -> o d", o=1).to_broadcast([P, EXPERTS])),
                         (w_gate[:], T["Wg"].rearrange("e d f -> d e f")), (w_up[:], T["Wu"].rearrange("e d f -> d e f"))):
            back_w = load(dst, src, "dma_back_weights")
        for j, (f, n) in enumerate(F_TILES):
            back_w = load(w_down[:n, :, j, :], T["Wd"][:, f:f + n, :].rearrange("e f d -> f e d"), "dma_back_weights")
        load_x(2)

        op("vector", "halved", lambda e: e.tensor_scalar(w_in[:, D_INNER:], w_in[:, D_INNER:], 0.5, None, ALU.mult), [front_w])
        op("vector", "halved", lambda e: e.tensor_scalar(w_conv[:], w_conv[:], 0.5, None, ALU.mult))
        front_ready = op("vector", "halved", lambda e: e.tensor_scalar(b_conv[:], b_conv[:], 0.5, None, ALU.mult))
        a_exp = op("scalar", "a_exp", lambda e: e.activation(a_neg[:], a_neg[:], ACT.Exp), [front_w])
        a_ready = op("vector", "a_ready", lambda e: e.tensor_scalar(a_neg[:], a_neg[:], -1.0, None, ALU.mult), [a_exp])
        half_made = op("gpsimd", "half_made", lambda e: e.memset(minus_half[:], -0.5))
        zero0 = op("vector", "halo_zero", lambda e: e.memset(x_in[:, 0, :, 0:HALO], 0.0))
        back_ready = {}

        def halve_back():
            op("gpsimd", "back_halved", lambda e: e.tensor_scalar(w_ffg[:, :D_MODEL], w_ffg[:, :D_MODEL], 0.5, None, ALU.mult), [back_w])
            op("gpsimd", "back_halved", lambda e: e.tensor_scalar(b_ffg[:, 0:1], b_ffg[:, 0:1], 0.5, None, ALU.mult))
            back_ready[0] = op("gpsimd", "back_halved", lambda e: e.tensor_scalar(w_gate[:], w_gate[:], 0.5, None, ALU.mult))

        last = {}

        def norm(src, dst, slot, after, free):
            for s in range(SUB):
                st = op("vector", "stats", lambda e, s=s: e.bn_stats(stats[:, s, :], src[:, s, :]), list(after) + [last.get("normed")])
            for s in range(SUB):
                ag = op("vector", "aggr", lambda e, s=s: e.bn_aggr(mean_var[:, slot, s, :], stats[:, s, :]), [st])
            ve = op("gpsimd", "rstd", lambda e: e.tensor_scalar(rstd[:, slot, :], mean_var[:, slot, :, 1], EPS, None, ALU.add), [ag])
            rs = op("gpsimd", "rstd", lambda e: e.tensor_tensor(rstd[:, slot, :], rstd[:, slot, :], minus_half[:], ALU.pow), [ve, half_made])
            for s in range(SUB):
                done = op("vector", "normed", lambda e, s=s: e.tensor_scalar(
                    dst[:, s, :], src[:, s, :], mean_var[:, slot, s, 0:1], rstd[:, slot, s:s + 1],
                    ALU.subtract, ALU.mult), [rs] + list(free))
            last["normed"] = done
            return done

        def transposes(src, after):
            g, free = work()
            for s in range(SUB):
                tok = op("tensor", "transposed", lambda e, s=s, g=g: e.transpose(
                    work_bank[g][:, s * P:(s + 1) * P], src[:, s, :], ident[:]), list(after) + [free])
            return g, tok

        x_one_ready, xc_ready, z_ready, scan_in_ready, stack_ready = {}, {}, {}, {}, {}
        y_done, d_read, du_read, stack_read, xin_done = {}, {}, {}, {}, {}
        xc_free, z_free, x_one_free, x_free = {}, {}, {}, {}

        def front(c):
            sx, s2 = c % 3, c % 2
            t = norm(x_tok[:, sx], x_one[:, sx], 0, [x_loaded[c]], [x_one_free.get(c - 3)])
            x_one_ready[c] = t
            yield
            t = norm(x_one[:, sx], u_tok, 1, [t], [last.get("u_tok")])
            yield
            g, t = transposes(u_tok, [t, front_w])
            last["u_tok"] = t
            t = op("scalar", "u_t", lambda e, g=g: e.activation(u_t[:], work_bank[g][:], ACT.Identity,
                                                          bias=norm_gb[:, 1:2], scale=norm_gb[:, 0:1]), [t, last.get("u_t"), front_w])
            release(g, t)
            u_ready = t
            yield
            cps = []
            for h in range(HALVES):
                g, free = work()
                mm = op("tensor", "in_proj", lambda e, h=h, g=g: e.matmul(
                    work_bank[g][:], w_in[:, h * P:(h + 1) * P], u_t[:], start=True, stop=True), [u_ready, free, front_ready])
                cp = op("scalar", "x_in", lambda e, h=h, g=g: e.activation(
                    x_in[:, s2, h, HALO:], work_bank[g][:], ACT.Copy), [mm, xin_done.get(c - 2)])
                release(g, cp)
                cps.append(cp)
            yield
            if c % (SEQ // CHUNK) == 0:
                halo = zero0 if c == 0 else op("vector", "halo_zero", lambda e: e.memset(x_in[:, s2, :, 0:HALO], 0.0), [xin_done.get(c - 2)])
            else:
                halo = op("vector", "halo", lambda e: e.tensor_copy(x_in[:, s2, :, 0:HALO], x_in[:, 1 - s2, :, CHUNK:]), [last["x_in"], xin_done.get(c - 2)])
            last["x_in"] = cps[-1]
            zs = []
            for h in range(HALVES):
                g, free = work()
                mm = op("tensor", "in_proj", lambda e, h=h, g=g: e.matmul(
                    work_bank[g][:], w_in[:, D_INNER + h * P:D_INNER + (h + 1) * P], u_t[:], start=True, stop=True), [free])
                th = op("scalar", "tanh_z", lambda e, g=g: e.activation(tanh_z[:], work_bank[g][:], ACT.Tanh), [mm, last.get("tanh_z")])
                z = op("vector", "silu_z", lambda e, h=h, g=g: e.scalar_tensor_tensor(
                    silu_z[:, s2, h, :], tanh_z[:], 1.0, work_bank[g][:], ALU.add, ALU.mult), [th, z_free.get(c - 2)])
                last["tanh_z"] = release(g, z)
                zs.append(z)
                yield
            last["u_t"] = mm
            z_ready[c] = zs[-1]
            for h in range(HALVES):
                t = op("scalar", "conv0", lambda e, h=h: e.activation(
                    conv[:, h, :], x_in[:, s2, h, 0:CHUNK], ACT.Identity, bias=b_conv[:, h:h + 1], scale=w_conv[:, h, 0:1]),
                    [halo, cps[h], last.get("conv"), front_ready])
                for k in range(1, D_CONV):
                    t = op("vector", "conv", lambda e, h=h, k=k: e.scalar_tensor_tensor(
                        conv[:, h, :], x_in[:, s2, h, k:k + CHUNK], w_conv[:, h, k:k + 1], conv[:, h, :], ALU.mult, ALU.add), [t])
                yield
            xin_done[c] = t
            th = op("scalar", "tanh_c", lambda e: e.activation(tanh_c[:], conv[:], ACT.Tanh), [t, last.get("tanh_c")])
            yield
            t = op("vector", "xc", lambda e: e.scalar_tensor_tensor(
                xc[:, s2], tanh_c[:], 1.0, conv[:], ALU.add, ALU.mult), [th, xc_free.get(c - 2)])
            xc_ready[c] = t
            yield
            g, free = work()
            for h in range(HALVES):
                mm = op("tensor", "x_proj", lambda e, h=h, g=g: e.matmul(
                    work_bank[g][0:PARTS * BC + DT_RANK, :], w_xproj[:, h, :], xc[:, s2, h, :],
                    start=h == 0, stop=h == HALVES - 1), [t, free])
            rows, dt_rows = slice(0, PARTS * BC), slice(PARTS * BC, PARTS * BC + DT_RANK)
            cp = op("scalar", "dt_low", lambda e, g=g: e.activation(dt_low[dt_rows, :], work_bank[g][dt_rows, :], ACT.Copy), [mm, last.get("dt_low")])
            t = op("scalar", "part", lambda e, g=g: e.activation(bc_part[:], work_bank[g][rows, :], ACT.Copy), [mm, last.get("bc")])
            t = op("vector", "rest", lambda e, g=g: e.scalar_tensor_tensor(
                bc_rest[:, 0, :], bc_part[:], part_mask[:, 0:1], work_bank[g][rows, :], ALU.mult, ALU.add), [t])
            release(g, t)
            yield
            t = op("scalar", "part", lambda e: e.activation(bc_part[:], bc_rest[:, 0, :], ACT.Copy), [t])
            t = op("vector", "rest", lambda e: e.scalar_tensor_tensor(
                bc_rest[:, 1, :], bc_part[:], part_mask[:, 1:2], bc_rest[:, 0, :], ALU.mult, ALU.add), [t])
            yield
            t = op("scalar", "part", lambda e: e.activation(bc_stack[:, s2, :], bc_rest[:, 1, :], ACT.Copy), [t, stack_read.get(c - 2)])
            stack_ready[c] = last["bc"] = t
            for h in range(HALVES):
                g, free = work()
                mm = op("tensor", "dt_proj", lambda e, h=h, g=g: e.matmul(
                    work_bank[g][:], w_dt[dt_rows, h * P:(h + 1) * P], dt_low[dt_rows, :], start=True, stop=True), [cp, free])
                t = op("scalar", "pre_dt", lambda e, h=h, g=g: e.activation(
                    pre_dt[:, h, :], work_bank[g][:], ACT.Identity, bias=b_dt[:, h:h + 1]), [mm, last.get("pre_dt")])
                release(g, t)
            last["dt_low"] = mm
            yield
            t = op("scalar", "abs_dt", lambda e: e.activation(exp_dt[:], pre_dt[:], ACT.Abs), [t])
            z = op("scalar", "exp_dt", lambda e: e.activation(exp_dt[:], exp_dt[:], ACT.Exp, scale=-1.0), [t])
            yield
            ln = op("scalar", "log_dt", lambda e: e.activation(log_dt[:], exp_dt[:], ACT.Ln, bias=1.0), [z])
            t = op("vector", "series", lambda e: e.tensor_scalar(ser_dt[:], exp_dt[:], 0.2, -0.25, ALU.mult, ALU.add), [z])
            for k in (0.0, 1.0 / 3.0, -0.5, 1.0):
                t = op("vector", "series", lambda e, k=k: e.scalar_tensor_tensor(
                    ser_dt[:], ser_dt[:], k, exp_dt[:], ALU.add, ALU.mult), [t])
            yield
            mk = op("vector", "small", lambda e: e.tensor_scalar(small[:], exp_dt[:], 2.0 ** -5, None, ALU.is_lt), [t])
            last["conv"] = last["tanh_c"] = mk
            t = op("vector", "log1p", lambda e: e.copy_predicated(log_dt[:], small[:], ser_dt[:]), [mk, ln])
            yield
            t = op("vector", "delta", lambda e: e.scalar_tensor_tensor(
                delta[:, s2], pre_dt[:], 0.0, log_dt[:], ALU.max, ALU.add), [t, d_read.get(c - 2)])
            last["pre_dt"] = last["conv"] = last["tanh_c"] = t
            t = op("vector", "du", lambda e: e.tensor_tensor(du[:, s2], delta[:, s2], xc[:, s2], ALU.mult), [t, du_read.get(c - 2)])
            scan_in_ready[c] = t
            yield

        inflow_ready, b_copied, scanned, multiplied, summed, carried = {}, {}, {}, {}, {}, {}
        units = [(c, n) for c in range(CHUNKS) for n in range(D_STATE)]
        last_y_read = {}

        def prepare(i):
            if i >= len(units):
                return
            c, n = units[i]
            s2 = c % 2
            mm = op("tensor", "b_row", lambda e: e.matmul(b_bank[:], select_row[:, n, :], bc_stack[:, s2, :], start=True, stop=True),
                    [stack_ready[c], b_copied.get(i - 1)])
            b_copied[i] = op("scalar", "b_wide", lambda e: e.activation(b_wide[:, i % 3, :], b_bank[:], ACT.Copy), [mm, inflow_ready.get(i - 3)])
            inflow_ready[i] = op("gpsimd", "inflow", lambda e: e.tensor_tensor(
                inflow[:, i % 3], du[:, s2], b_wide[:, i % 3:i % 3 + 1, :].to_broadcast([P, HALVES, CHUNK]), ALU.mult),
                [b_copied[i], scan_in_ready[c], scanned.get(i - 3)])
            du_read[c] = inflow_ready[i]

        def scan(i):
            c, n = units[i]
            s2 = c % 2
            mm = op("tensor", "c_row", lambda e: e.matmul(c_bank[:], select_row[:, D_STATE + n, :], bc_stack[:, s2, :], start=True, stop=True),
                    [stack_ready[c], multiplied.get(i - 1)])
            stack_read[c] = mm
            first = c % (SEQ // CHUNK) == 0
            for h in range(HALVES):
                ex = op("scalar", "decay", lambda e, h=h: e.activation(
                    decay_bank[h][:], delta[:, s2, h, :], ACT.Exp, scale=a_neg[:, h, n:n + 1]),
                    [scan_in_ready[c], a_ready, scanned.get((i - 1, h))])
                d_read[c] = ex
                initial = 0.0 if first else carry[:, n, h:h + 1]
                scanned[(i, h)] = op("vector", "scanned", lambda e, h=h, initial=initial: e.tensor_tensor_scan(
                    state[:, i % 2, h, :], decay_bank[h][:], inflow[:, i % 3, h, :], initial, ALU.mult, ALU.add),
                    [ex, inflow_ready[i], multiplied.get(i - 2), carried.get(i - 2), carried.get(i - D_STATE)])
            scanned[i] = scanned[(i, HALVES - 1)]
            carried[i] = op("gpsimd", "carried", lambda e: e.tensor_copy(carry[:, n, :], state[:, i % 2, :, CHUNK - 1]), [scanned[i]])
            multiplied[i] = op("vector", "times_c", lambda e: e.tensor_tensor(
                prod[:, i % 2], state[:, i % 2], c_bank[:].rearrange("p (o t) -> p o t", o=1).to_broadcast([P, HALVES, CHUNK]), ALU.mult),
                [scanned[i], mm, summed.get(i - 2)])

        def total(i):
            if i < 0:
                return
            c, n = units[i]
            for h in range(HALVES):
                summed[i] = op("tensor", "y_sum", lambda e, h=h: e.matmul(
                    y_bank[h][:], ident[:], prod[:, i % 2, h, :], start=n == 0, stop=n == D_STATE - 1),
                    [multiplied[i], last_y_read.get((c - 1, h))])
            if n == D_STATE - 1:
                y_done[c] = summed[i]

        def take_y(c):
            s2 = c % 2
            for h in range(HALVES):
                t = op("vector", "y_skip", lambda e, h=h: e.scalar_tensor_tensor(
                    y_gated[:, h, :], xc[:, s2, h, :], skip_d[:, h:h + 1], y_bank[h][:], ALU.mult, ALU.add),
                    [y_done[c], last.get("y_gated")])
                last_y_read[(c, h)] = t
            xc_free[c] = t
            t = op("vector", "y_gate", lambda e: e.tensor_tensor(y_gated[:], y_gated[:], silu_z[:, s2], ALU.mult), [t])
            z_free[c] = last["y_gate"] = t

        def back(c):
            sx, s2 = c % 3, c % 2
            g, free = work()
            for s in range(SUB):
                for h in range(HALVES):
                    mm = op("tensor", "out_proj", lambda e, s=s, h=h, g=g: e.matmul(
                        work_bank[g][:, s * P:(s + 1) * P], y_gated[:, h, s * P:(s + 1) * P], w_out[:, h, :],
                        start=h == 0, stop=h == HALVES - 1), [last["y_gate"], free, back_w])
            last["y_gated"] = mm
            t = op("vector", "x_two", lambda e, g=g: e.tensor_tensor(
                x_two[:], x_one[:, sx], work_bank[g][:].rearrange("p (s d) -> p s d", s=SUB), ALU.add), [mm, x_one_ready[c]])
            x_one_free[c] = release(g, t)
            x2 = t
            xb = op("gpsimd", "x_plus_b", lambda e: e.tensor_tensor(
                x_tok[:, sx], x_tok[:, sx], b_ffp[:].rearrange("p (o d) -> p o d", o=1).to_broadcast([P, SUB, D_MODEL]), ALU.add), [x_one_ready[c], back_w])
            yield
            t = norm(x_two, n_tok, 2, [t], [last.get("n_tok")])
            yield
            g, t = transposes(n_tok, [t])
            last["n_tok"] = t
            t = op("scalar", "n_t", lambda e, g=g: e.activation(n_t[:], work_bank[g][:], ACT.Identity,
                                                              bias=norm_gb[:, 3:4], scale=norm_gb[:, 2:3]), [t, last.get("n_t")])
            release(g, t)
            yield
            g, free = work()
            mm = op("tensor", "ff_gate", lambda e, g=g: e.matmul(work_bank[g][:], w_ffg[:, 0:P], n_t[:], start=True, stop=True),
                    [t, free, back_ready[0]])
            th = op("scalar", "tanh_g", lambda e, g=g: e.activation(tanh_g[:], work_bank[g][:], ACT.Tanh, bias=b_ffg[:, 0:1]), [mm, last.get("gate_h")])
            t = op("scalar", "gate_h", lambda e, g=g: e.activation(gate_h[:], work_bank[g][:], ACT.Identity, bias=b_ffg[:, 0:1]), [mm])
            release(g, t)
            yield
            g, free = work()
            mm = op("tensor", "ff_val", lambda e, g=g: e.matmul(work_bank[g][:], w_ffg[:, P:], n_t[:], start=True, stop=True), [free])
            last["n_t"] = mm
            t = op("vector", "silu_g", lambda e: e.scalar_tensor_tensor(gate_h[:], tanh_g[:], 1.0, gate_h[:], ALU.add, ALU.mult), [t, th])
            t = op("vector", "ff_h", lambda e, g=g: e.scalar_tensor_tensor(
                ff_h[:], work_bank[g][:], b_ffg[:, 1:2], gate_h[:], ALU.add, ALU.mult), [t, mm, last.get("ff_h")])
            last["gate_h"] = release(g, t)
            yield
            g, free = work()
            for s in range(SUB):
                mm = op("tensor", "ff_out", lambda e, s=s, g=g: e.matmul(
                    work_bank[g][:, s * P:(s + 1) * P], ff_h[:, s * P:(s + 1) * P], w_ffp[:], start=True, stop=True), [t, free])
            last["ff_h"] = mm
            t = op("vector", "x_three", lambda e, g=g: e.tensor_tensor(
                x_two[:], x_two[:], work_bank[g][:].rearrange("p (s d) -> p s d", s=SUB), ALU.add), [mm])
            release(g, t)
            t = op("vector", "x_four", lambda e: e.tensor_tensor(x_four[:, s2], x_two[:], x_tok[:, sx], ALU.add), [t, xb, out_sent.get(c - 2)])
            x_free[c] = t
            yield
            t = norm(x_four[:, s2], m_tok, 3, [t], [last.get("m_tok")])
            yield
            g, t = transposes(m_tok, [t])
            last["m_tok"] = t
            t = op("scalar", "m_t", lambda e, g=g: e.activation(m_t[:, s2, :], work_bank[g][:], ACT.Copy), [t, last.get(("moe", c - 2))])
            release(g, t)
            m_ready = t
            yield
            g, free = work()
            for s in range(SUB):
                mm = op("tensor", "route", lambda e, s=s, g=g: e.matmul(
                    work_bank[g][:, s * EXPERTS:(s + 1) * EXPERTS], m_t[:, s2, s * P:(s + 1) * P], w_route[:], start=True, stop=True), [t, free])
            t = op("vector", "route_v", lambda e, g=g: e.tensor_tensor(
                logits[:], work_bank[g][:, :SUB * EXPERTS].rearrange("p (s e) -> p s e", s=SUB),
                b_route[:].rearrange("p (o e) -> p o e", o=1).to_broadcast([P, SUB, EXPERTS]), ALU.add), [mm])
            release(g, t)
            for s in range(SUB):
                mx = op("vector", "route_v", lambda e, s=s: e.max(top8[:, s, :], logits[:, s, :]), [t])
            for s in range(SUB):
                ix = op("vector", "route_v", lambda e, s=s: e.max_index(top_i[:, s, :], top8[:, s, :], logits[:, s, :]), [mx])
            gap = op("vector", "route_v", lambda e: e.tensor_tensor(top_w[:, 0, :], top8[:, :, 1], top8[:, :, 0], ALU.subtract), [ix])
            t = op("vector", "route_v", lambda e: e.tensor_copy(top_if[:], top_i[:]), [ix])
            ex = op("scalar", "route_exp", lambda e: e.activation(top_w[:, 1, :], top_w[:, 0, :], ACT.Exp), [gap])
            yield
            t2 = op("vector", "route_v", lambda e: e.tensor_scalar(top_w[:, 2, :], top_w[:, 1, :], 1.0, None, ALU.add), [ex])
            t2 = op("vector", "route_v", lambda e: e.reciprocal(top_w[:, 2, :], top_w[:, 2, :]), [t2])
            t2 = op("vector", "route_v", lambda e: e.tensor_tensor(top_w[:, 3, :], top_w[:, 1, :], top_w[:, 2, :], ALU.mult), [t2])
            for s in range(SUB):
                t = op("vector", "route_v", lambda e, s=s: e.tensor_scalar(
                    combine[:, s2, s, :], iota8[:], top_if[:, s, 0:1], top_w[:, 2, s:s + 1], ALU.is_equal, ALU.mult), [t2, last.get(("moe", c - 2))])
                t = op("vector", "route_v", lambda e, s=s: e.tensor_scalar(
                    hot[:, s, :], iota8[:], top_if[:, s, 1:2], top_w[:, 3, s:s + 1], ALU.is_equal, ALU.mult), [t2])
            cmb = op("vector", "route_v", lambda e: e.tensor_tensor(combine[:, s2], combine[:, s2], hot[:], ALU.add), [t])
            yield
            for x in range(EXPERTS):
                hs = []
                for j, (f, n) in enumerate(F_TILES):
                    gg, free = work()
                    mg = op("tensor", "moe_gate", lambda e, gg=gg, f=f, n=n, x=x: e.matmul(
                        work_bank[gg][:n, :], w_gate[:, x, f:f + n], m_t[:, s2, :], start=True, stop=True), [m_ready, free, back_ready[0]])
                    th = op("scalar", "tanh_m", lambda e, gg=gg, n=n, j=j: e.activation(
                        tanh_m[:n, :], work_bank[gg][:n, :], ACT.Tanh), [mg, last.get("tanh_m")])
                    gu, free = work()
                    mu = op("tensor", "moe_up", lambda e, gu=gu, f=f, n=n, x=x: e.matmul(
                        work_bank[gu][:n, :], w_up[:, x, f:f + n], m_t[:, s2, :], start=True, stop=True), [free])
                    t = op("vector", "moe_silu", lambda e, gg=gg, n=n: e.scalar_tensor_tensor(
                        half_m[:n, :], tanh_m[:n, :], 1.0, work_bank[gg][:n, :], ALU.add, ALU.mult), [th, last.get("half_m")])
                    last["tanh_m"] = release(gg, t)
                    t = op("vector", "moe_h", lambda e, gu=gu, n=n, j=j, x=x: e.tensor_tensor(
                        h_moe[:n, j, :], half_m[:n, :], work_bank[gu][:n, :], ALU.mult), [t, mu, last.get("down")])
                    last["half_m"] = release(gu, t)
                    yield
                g, free = work()
                for s in range(SUB):
                    for j, (f, n) in enumerate(F_TILES):
                        mm = op("tensor", "moe_down", lambda e, g=g, s=s, j=j, n=n, x=x: e.matmul(
                            work_bank[g][:, s * P:(s + 1) * P], h_moe[:n, j, s * P:(s + 1) * P], w_down[:n, x, j, :],
                            start=j == 0, stop=j == NF - 1), [t, free])
                last["down"] = mm
                for s in range(SUB):
                    t = op("vector", "moe_add", lambda e, g=g, s=s, x=x: e.scalar_tensor_tensor(
                        x_four[:, s2, s, :], work_bank[g][:, s * P:(s + 1) * P], combine[:, s2, s, x:x + 1], x_four[:, s2, s, :],
                        ALU.mult, ALU.add), [mm, cmb, last.get("acc")])
                last["acc"] = release(g, t)
            last[("moe", c)] = t
            out_sent[c] = op("sync", f"dma_out{s2}", lambda e: e.dma_start(out_dram[c], x_four[:, s2]), [t])
            yield

        for _ in front(0):
            pass
        halve_back()
        for i in range(3):
            prepare(i) if i < 2 else None
        for c in range(CHUNKS):
            side = []
            if c + 1 < CHUNKS:
                if c + 1 >= 3:
                    load_x(c + 1, [x_free[c - 2]])
                f = list_steps(front(c + 1))
                side.append(f)
            if c >= 1:
                side.append(list_steps(back(c - 1)))
            for n in range(D_STATE):
                i = c * D_STATE + n
                if n == D_STATE - 2:
                    drain(side[:1] if c + 1 < CHUNKS else [])
                prepare(i + 2)
                scan(i)
                total(i - 1) if n else None
                for k, s in enumerate(side):
                    per = 2 if (k == 0 and c + 1 < CHUNKS) else 3
                    for _ in range(per):
                        next(s, None)
            total(c * D_STATE + D_STATE - 1)
            drain(side)
            take_y(c)
        for _ in back(CHUNKS - 1):
            pass
        pr.wait("sync", [out_sent[CHUNKS - 2], out_sent[CHUNKS - 1]])

        block = ctx.enter_context(nc.Block())

        @block.sync
        def _(eng):
            pr.play("sync", eng)

        @block.gpsimd
        def _(eng):
            pr.play("gpsimd", eng)

        @block.scalar
        def _(eng):
            pr.play("scalar", eng)

        @block.vector
        def _(eng):
            pr.play("vector", eng)

        @block.tensor
        def _(eng):
            pr.play("tensor", eng)


def list_steps(gen):
    return gen


def drain(gens):
    for g in gens:
        for _ in g:
            pass


def shape_constants():
    ident = np.eye(P, dtype=np.float32)
    rows = np.arange(PARTS * BC)
    select = np.zeros((PARTS * BC, BC, P), np.float32)
    select[rows, rows % BC, :] = 1.0
    mask = -np.stack([rows >= BC, rows >= 2 * BC], 1).astype(np.float32)
    iota8 = np.tile(np.arange(EXPERTS, dtype=np.float32), (P, 1))
    return ident, select, mask, iota8


def columns(vector):
    return vector.reshape(-1, P).T


def kernel(**inputs):
    import concourse.bacc as bacc
    import ml_dtypes
    from concourse.bass_utils import run_bass_kernel_spmd as run

    a = {k.replace("L0_attn_", "").replace("L0_ffn_", ""): np.asarray(v) for k, v in inputs.items()}
    ident, select, mask, iota8 = shape_constants()
    xproj = a["x_proj_w"]
    dt_rows, bc_rows = xproj[:DT_RANK], xproj[DT_RANK:]
    arrays = {
        "x": a["x"], "ident": ident, "select_row": select.astype(ml_dtypes.bfloat16), "part_mask": mask, "iota8": iota8,
        "in_wT": a["in_proj_w"].T, "norm_gb": np.stack([a["n1_g"], a["n1_b"], a["n2_g"], a["n2_b"]], 1),
        "conv_w": a["conv_w"], "conv_b": columns(a["conv_b"]),
        "xproj_wT": np.concatenate([bc_rows] * PARTS + [dt_rows], 0).T,
        "dt_wT": a["dt_w"].T, "dt_b": columns(a["dt_b"]), "A_log": a["A_log"], "D": columns(a["D"]), "out_wT": a["out_w"].T,
        "ffg_wT": a["ffg_w"].T, "ffg_b": columns(a["ffg_b"]), "ffp_wT": a["ffp_w"].T, "ffp_b": a["ffp_b"],
        "Ws": a["Ws"], "bs": a["bs"], "Wg": a["Wg"], "Wu": a["Wu"], "Wd": a["Wd"],
    }
    nc = bacc.Bacc("TRN2", target_bir_lowering=False, num_devices=1)
    feeds, T = {}, {}
    for name, array in arrays.items():
        array = np.ascontiguousarray(array)
        feeds[f"in_{name}"] = array
        T[name] = nc.dram_tensor(f"in_{name}", array.shape, mybir.dt.from_np(array.dtype), kind="ExternalInput").ap()
    out = nc.dram_tensor("out_0", (BATCH, SEQ, D_MODEL), mybir.dt.float32, kind="ExternalOutput").ap()
    mamba_moe_block(nc, T, out)
    result = run(nc, [feeds], core_ids=[0])
    return result.results[0]["out_0"]
```

```python
from contextlib import ExitStack

import numpy as np

import concourse.bass as bass
from concourse import mybir

BATCH, SEQ, D_MODEL = 2, 2048, 128
TOKENS = BATCH * SEQ
D_INNER, D_STATE, D_CONV, DT_RANK = 256, 16, 4, 8
HALVES = D_INNER // 128
EXPERTS, FF = 8, 344
EPS = 1e-5
P = 128
CHUNK = 512
SUB = CHUNK // P
CHUNKS = TOKENS // CHUNK
TOPK = 2
GROUPS = [range(0, 3), range(3, 5), range(5, 8)]
TILES = [(TOPK * CHUNK * len(g) - EXPERTS) // P + EXPERTS for g in GROUPS]
HALO = D_CONV - 1
BC = 2 * D_STATE
ROW_SLOTS = 3
F_TILES = [(f, min(P, FF - f)) for f in range(0, FF, P)]
NF = len(F_TILES)
FRONT, SIDE = 0, 1


class Program:

    def __init__(self, nc, ctx):
        self.nc, self.ctx = nc, ctx
        self.queue = {e: [] for e in ("sync", "gpsimd", "scalar", "vector", "tensor")}
        self.sems, self.count, self.seen = {}, {}, {}

    def op(self, engine, done, build, after=()):
        step = 16 if done.startswith("dma_") else 1
        if done not in self.sems:
            self.sems[done] = self.ctx.enter_context(self.nc.semaphore(done))
            self.count[done] = 0
        waits = []
        for token in after:
            if token is None:
                continue
            name, value = token
            if self.seen.get((engine, name), 0) < value:
                self.seen[(engine, name)] = value
                waits.append((self.sems[name], value))
        self.count[done] += step
        self.queue[engine].append((waits, build, self.sems[done], step))
        return (done, self.count[done])

    def wait(self, engine, after):
        waits = [(self.sems[n], v) for n, v in after]
        self.queue[engine].append((waits, None, None, 0))

    def play(self, engine, eng):
        for waits, build, sem, step in self.queue[engine]:
            for s, v in waits:
                eng.wait_ge(s, v)
            if build is not None:
                build(eng).then_inc(sem, step)


def mamba_moe_block(nc, T, out):
    f32, bf16, u32, i32 = mybir.dt.float32, mybir.dt.bfloat16, mybir.dt.uint32, mybir.dt.int32
    ALU, ACT, AX = mybir.AluOpType, mybir.ActivationFunctionType, mybir.AxisListType
    ctx = ExitStack()
    with ctx:
        def sb(name, shape, dt=f32):
            return ctx.enter_context(nc.sbuf_tensor(name, shape, dt))

        def bank(name):
            return ctx.enter_context(nc.psum_tensor(name, [P, CHUNK], f32))

        pr = Program(nc, ctx)

        ident = sb("ident", [P, P])
        iota8 = sb("iota8", [P, EXPERTS])
        iota_tile = sb("iota_tile", [P, max(TILES)])
        before = sb("before", [P, P])
        ones = sb("ones", [P, P])
        token_id = sb("token_id", [P, TOKENS // P])
        iota_p = sb("iota_p", [P, P])
        w_in = sb("w_in", [P, 2 * D_INNER])
        w_conv = sb("w_conv", [P, HALVES, D_CONV])
        b_conv = sb("b_conv", [P, HALVES])
        w_xproj = sb("w_xproj", [P, HALVES, BC + DT_RANK])
        w_dt = sb("w_dt", [P, D_INNER])
        b_dt = sb("b_dt", [P, HALVES])
        a_neg = sb("a_neg", [P, HALVES, D_STATE])
        skip_d = sb("skip_d", [P, HALVES])
        diag_d = sb("diag_d", [P, HALVES, P])
        w_out = sb("w_out", [P, HALVES, D_MODEL])
        norm_gb = sb("norm_gb", [P, 4])
        w_ffg = sb("w_ffg", [P, 2 * D_MODEL])
        b_ffg = sb("b_ffg", [P, 2])
        w_ffp = sb("w_ffp", [P, D_MODEL])
        b_ffp = sb("b_ffp", [P, D_MODEL])
        w_route = sb("w_route", [P, EXPERTS])
        b_route = sb("b_route", [P, EXPERTS])
        w_gate = sb("w_gate", [P, EXPERTS, FF])
        w_up = sb("w_up", [P, EXPERTS, FF])
        w_down = sb("w_down", [P, EXPERTS, NF, D_MODEL])

        x_tok = sb("x_tok", [P, CHUNKS, SUB, D_MODEL])
        x_one = sb("x_one", [P, 3, SUB, D_MODEL])
        u_tok = sb("u_tok", [P, SUB, D_MODEL])
        u_t = sb("u_t", [P, CHUNK])
        x_in = sb("x_in", [P, 2, HALVES, HALO + CHUNK])
        conv = sb("conv", [P, HALVES, CHUNK])
        tanh_c = sb("tanh_c", [P, HALVES, CHUNK])
        xc = sb("xc", [P, 2, HALVES, CHUNK])
        silu_z = sb("silu_z", [P, 2, HALVES, CHUNK])
        x_dbl = sb("x_dbl", [BC + DT_RANK, CHUNK])
        exp_dt, ser_dt = tanh_c, conv
        delta = sb("delta", [P, 2, HALVES, CHUNK])
        du = sb("du", [P, 2, HALVES, CHUNK])
        b_wide = sb("b_wide", [P, ROW_SLOTS, CHUNK])
        c_wide = sb("c_wide", [P, ROW_SLOTS, CHUNK])
        inflow = sb("inflow", [P, 3, HALVES, CHUNK])
        state = sb("state", [P, 2, HALVES, CHUNK])
        carry = sb("carry", [P, D_STATE, HALVES])
        prod = sb("prod", [P, 2, HALVES, CHUNK])
        y_gated = sb("y_gated", [P, HALVES, CHUNK])
        x_two = sb("x_two", [P, SUB, D_MODEL])
        n_tok = sb("n_tok", [P, SUB, D_MODEL])
        n_t = sb("n_t", [P, CHUNK])
        tanh_g = sb("tanh_g", [P, CHUNK])
        gate_h = sb("gate_h", [P, CHUNK])
        ff_h = gate_h
        m_tok = sb("m_tok", [P, SUB, D_MODEL])
        m_t = sb("m_t", [P, CHUNK])
        logits = sb("logits", [P, SUB, EXPERTS])
        top8 = sb("top8", [P, SUB, 8])
        top_i = sb("top_i", [P, SUB, 8], u32)
        top_if = sb("top_if", [P, SUB, 8])
        top_w = sb("top_w", [P, 2, SUB])
        both = sb("both", [P, SUB, EXPERTS])
        tile_sum = sb("tile_sum", [P, 2, SUB, EXPERTS])
        choice_w = sb("choice_w", [P, TOPK, TOKENS // P])
        choice = sb("choice", [P, TOPK, TOKENS // P, EXPERTS])
        rank = sb("rank", [P, TOKENS // P, EXPERTS])
        count = sb("count", [P, 2, EXPERTS])
        tiles_i = sb("tiles_i", [P, EXPERTS], i32)
        tiles_f = sb("tiles_f", [P, EXPERTS])
        tiles_end = sb("tiles_end", [P, EXPERTS])
        start = sb("start", [P, EXPERTS])
        passed = sb("passed", [P, max(TILES), EXPERTS])
        expert_f = sb("expert_f", [P, max(TILES)])
        expert_i = sb("expert_i", [P, len(GROUPS), max(TILES)], i32)
        picked = sb("picked", [P, TOKENS // P, EXPERTS])
        place_f = sb("place_f", [P, TOKENS // P])
        place = sb("place", [P, TOPK, TOKENS // P], u32)
        place_lo = sb("place_lo", [P, TOKENS // P], i32)
        place_hi = sb("place_hi", [P, TOKENS // P], i32)
        place_lf = sb("place_lf", [P, TOPK, TOKENS // P])
        place_hf = sb("place_hf", [P, TOPK, TOKENS // P])
        hot_lo = sb("hot_lo", [P, 2, P])
        hot_hi = sb("hot_hi", [P, 2, max(TILES)])
        slot_token = sb("slot_token", [P, len(GROUPS), max(TILES)], u32)
        x_rows = sb("x_rows", [P, 3, D_MODEL])
        x_cols = sb("x_cols", [P, 2, P])
        silu_m = sb("silu_m", [P, FF])
        h_rows = sb("h_rows", [P, 2, FF])
        h_cols = sb("h_cols", [P, 2, NF, P])
        y_rows = sb("y_rows", [P, 2, D_MODEL])
        y_pair = sb("y_pair", [P, 2, TOPK, D_MODEL])
        var_one = sb("var_one", [P, SUB])
        stats = sb("stats", [P, SUB, 6])
        mean_var = sb("mean_var", [P, 4, SUB, 2])
        rstd = sb("rstd", [P, 4, SUB])
        minus_half = sb("minus_half", [P, SUB])

        decay_bank = [bank("decay0"), bank("decay1")]
        y_bank = [bank("y0"), bank("y1")]
        work_bank = [bank("work_front"), bank("work_side")]
        expert_bank = [bank("expert0"), bank("expert1")]
        work_free = [None, None]

        def work(g):
            return g, work_free[g]

        def release(g, token):
            work_free[g] = token
            return token

        op = pr.op

        def load(dst, src, name="dma_weights", engine="sync", after=()):
            return op(engine, name, lambda e: e.dma_start(dst, src), after)

        x_dram = T["x"].rearrange("b (c s p) d -> (b c) p s d", s=SUB, p=P)
        out_dram = out.rearrange("b (c s p) d -> (b c) p s d", s=SUB, p=P)
        x_loaded, out_sent = {}, {}

        def load_x(c, after=()):
            x_loaded[c] = load(x_tok[:, c], x_dram[c], f"dma_x{c}", after=after)

        load_x(0)
        load(ident[:], T["ident"])
        load(w_in[:], T["in_wT"])
        load(norm_gb[:], T["norm_gb"])
        load(w_conv[:], T["conv_w"].rearrange("(h p) o k -> p h (o k)", p=P))
        load(b_conv[:], T["conv_b"])
        load(w_xproj[:], T["xproj_wT"].rearrange("(h p) m -> p h m", p=P))
        load(w_dt[BC:BC + DT_RANK, :], T["dt_wT"])
        load(b_dt[:], T["dt_b"])
        load(a_neg[:], T["A_log"].rearrange("(h p) n -> p h n", p=P))
        front_w = load(skip_d[:], T["D"])
        load_x(1)
        for dst, src in ((w_out[:], T["out_wT"].rearrange("(h p) m -> p h m", p=P)), (w_ffg[:], T["ffg_wT"]),
                         (b_ffg[:], T["ffg_b"]), (w_ffp[:], T["ffp_wT"]),
                         (b_ffp[:], T["ffp_b"].rearrange("(o d) -> o d", o=1).to_broadcast([P, D_MODEL])),
                         (w_route[:], T["Ws"]), (iota8[:], T["iota8"]), (iota_tile[:], T["iota_tile"]), (before[:], T["before"]),
                         (token_id[:], T["token_id"]), (iota_p[:], T["iota_p"]),
                         (b_route[:], T["bs"].rearrange("(o d) -> o d", o=1).to_broadcast([P, EXPERTS])),
                         (w_gate[:], T["Wg"].rearrange("e d f -> d e f")), (w_up[:], T["Wu"].rearrange("e d f -> d e f"))):
            back_w = load(dst, src, "dma_back_weights")
        for j, (f, n) in enumerate(F_TILES):
            back_w = load(w_down[:n, :, j, :], T["Wd"][:, f:f + n, :].rearrange("e f d -> f e d"), "dma_back_weights")
        for c in range(2, CHUNKS):
            load_x(c)
        bc_dram = [nc.dram_tensor(f"bc_dram{c}", (BC, CHUNK), f32, kind="Internal").ap() for c in range(CHUNKS)]
        row_dram = [nc.dram_tensor(f"row_dram{k}", (CHUNK * len(g), D_MODEL), f32, kind="Internal").ap() for k, g in enumerate(GROUPS)]
        y_dram = [nc.dram_tensor(f"y_dram{k}", (P * n, D_MODEL), f32, kind="Internal").ap() for k, n in enumerate(TILES)]

        op("vector", "halved", lambda e: e.tensor_scalar(w_in[:, D_INNER:], w_in[:, D_INNER:], 0.5, None, ALU.mult), [front_w])
        op("vector", "halved", lambda e: e.tensor_scalar(w_conv[:], w_conv[:], 0.5, None, ALU.mult))
        front_ready = op("vector", "halved", lambda e: e.tensor_scalar(b_conv[:], b_conv[:], 0.5, None, ALU.mult))
        a_exp = op("scalar", "a_exp", lambda e: e.activation(a_neg[:], a_neg[:], ACT.Exp), [front_w])
        a_ready = op("vector", "a_ready", lambda e: e.tensor_scalar(a_neg[:], a_neg[:], -1.0, None, ALU.mult), [a_exp])
        for h in range(HALVES):
            diag_ready = op("vector", "diag_d", lambda e, h=h: e.tensor_scalar(diag_d[:, h, :], ident[:], skip_d[:, h:h + 1], None, ALU.mult), [front_w])
        half_made = op("gpsimd", "half_made", lambda e: e.memset(minus_half[:], -0.5))
        ones_made = op("gpsimd", "ones_made", lambda e: e.memset(ones[:], 1.0))
        zero0 = op("vector", "halo_zero", lambda e: e.memset(x_in[:, 0, :, 0:HALO], 0.0))
        back_ready = {}

        def halve_back():
            op("gpsimd", "back_halved", lambda e: e.tensor_scalar(w_ffg[:, :D_MODEL], w_ffg[:, :D_MODEL], 0.5, None, ALU.mult), [back_w])
            op("gpsimd", "back_halved", lambda e: e.tensor_scalar(b_ffg[:, 0:1], b_ffg[:, 0:1], 0.5, None, ALU.mult))
            back_ready[0] = op("gpsimd", "back_halved", lambda e: e.tensor_scalar(w_gate[:], w_gate[:], 0.5, None, ALU.mult))

        last = {}

        def norm(src, dst, slot, after, free):
            for s in range(SUB):
                st = op("vector", "stats", lambda e, s=s: e.bn_stats(stats[:, s, :], src[:, s, :]), list(after) + [last.get("aggr")])
            for s in range(SUB):
                ag = last["aggr"] = op("vector", "aggr", lambda e, s=s: e.bn_aggr(mean_var[:, slot, s, :], stats[:, s, :]), [st, last.get(("normed", slot))])
            yield
            t = rsqrt(slot, mean_var[:, slot, :, 1], [ag])
            yield
            last[("normed", slot)] = scaled(src, dst, slot, [t] + list(free))

        def rsqrt(slot, var, after):
            t = op("gpsimd", "rstd", lambda e: e.tensor_scalar(rstd[:, slot, :], var, EPS, None, ALU.add), after)
            return op("gpsimd", "rstd", lambda e: e.tensor_tensor(rstd[:, slot, :], rstd[:, slot, :], minus_half[:], ALU.pow), [t, half_made])

        def scaled(src, dst, slot, after):
            for s in range(SUB):
                t = op("vector", "normed", lambda e, s=s: e.tensor_scalar(
                    dst[:, s, :], src[:, s, :], mean_var[:, slot, s, 0:1], rstd[:, slot, s:s + 1],
                    ALU.subtract, ALU.mult), after)
            return t

        def transposes(g, src, after):
            g, free = work(g)
            for s in range(SUB):
                tok = op("tensor", "transposed", lambda e, s=s, g=g: e.transpose(
                    work_bank[g][:, s * P:(s + 1) * P], src[:, s, :], ident[:]), list(after) + [free])
            return g, tok

        x_one_ready, xc_ready, z_ready, scan_in_ready, bc_sent = {}, {}, {}, {}, {}
        y_done, d_read, du_read, xin_done = {}, {}, {}, {}
        xc_free, z_free, x_one_free, x_free = {}, {}, {}, {}

        def front(c):
            sx, s2 = c % 3, c % 2
            yield from norm(x_tok[:, c], x_one[:, sx], 0, [x_loaded[c]], [x_one_free.get(c - 3)])
            t = x_one_ready[c] = last[("normed", 0)]
            v = op("gpsimd", "var_one", lambda e: e.tensor_tensor(var_one[:], mean_var[:, 0, :, 1], rstd[:, 0, :], ALU.mult), [t, last.get("u_tok_made")])
            v = op("gpsimd", "var_one", lambda e: e.tensor_tensor(var_one[:], var_one[:], rstd[:, 0, :], ALU.mult), [v])
            v = rsqrt(1, var_one[:], [v])
            yield
            for s in range(SUB):
                t = op("vector", "u_tok", lambda e, s=s: e.tensor_scalar(
                    u_tok[:, s, :], x_one[:, sx, s, :], rstd[:, 1, s:s + 1], None, ALU.mult), [t, v, last.get("u_tok")])
            last["u_tok_made"] = t
            g, t = transposes(FRONT, u_tok, [t, front_w])
            last["u_tok"] = t
            yield
            t = op("scalar", "u_t", lambda e, g=g: e.activation(u_t[:], work_bank[g][:], ACT.Identity,
                                                          bias=norm_gb[:, 1:2], scale=norm_gb[:, 0:1]), [t, last.get("u_t"), front_w])
            release(g, t)
            u_ready = t
            cps = []
            for h in range(HALVES):
                g, free = work(FRONT)
                mm = op("tensor", "in_proj", lambda e, h=h, g=g: e.matmul(
                    work_bank[g][:], w_in[:, h * P:(h + 1) * P], u_t[:], start=True, stop=True), [u_ready, free, front_ready])
                yield
                cp = op("scalar", "x_in", lambda e, h=h, g=g: e.activation(
                    x_in[:, s2, h, HALO:], work_bank[g][:], ACT.Copy), [mm, xin_done.get(c - 2)])
                release(g, cp)
                cps.append(cp)
            yield
            if c % (SEQ // CHUNK) == 0:
                halo = zero0 if c == 0 else op("vector", "halo_zero", lambda e: e.memset(x_in[:, s2, :, 0:HALO], 0.0), [xin_done.get(c - 2)])
            else:
                halo = op("vector", "halo", lambda e: e.tensor_copy(x_in[:, s2, :, 0:HALO], x_in[:, 1 - s2, :, CHUNK:]), [last["x_in"], xin_done.get(c - 2)])
            last["x_in"] = cps[-1]
            for h in range(HALVES):
                t = op("scalar", "conv0", lambda e, h=h: e.activation(
                    conv[:, h, :], x_in[:, s2, h, 0:CHUNK], ACT.Identity, bias=b_conv[:, h:h + 1], scale=w_conv[:, h, 0:1]),
                    [halo, cps[h], last.get("conv"), front_ready])
                for k in range(1, D_CONV):
                    t = op("vector", "conv", lambda e, h=h, k=k: e.scalar_tensor_tensor(
                        conv[:, h, :], x_in[:, s2, h, k:k + CHUNK], w_conv[:, h, k:k + 1], conv[:, h, :], ALU.mult, ALU.add), [t])
                yield
            xin_done[c] = t
            th = op("scalar", "tanh_c", lambda e: e.activation(tanh_c[:], conv[:], ACT.Tanh), [t, last.get("tanh_c")])
            yield
            t = op("vector", "xc", lambda e: e.scalar_tensor_tensor(
                xc[:, s2], tanh_c[:], 1.0, conv[:], ALU.add, ALU.mult), [th, xc_free.get(c - 2)])
            xc_ready[c] = t
            g, free = work(FRONT)
            for h in range(HALVES):
                mm = op("tensor", "x_proj", lambda e, h=h, g=g: e.matmul(
                    work_bank[g][0:BC + DT_RANK, :], w_xproj[:, h, :], xc[:, s2, h, :],
                    start=h == 0, stop=h == HALVES - 1), [t, free])
            yield
            dt_rows = slice(BC, BC + DT_RANK)
            cp = release(g, op("scalar", "x_dbl", lambda e, g=g: e.activation(
                x_dbl[:], work_bank[g][0:BC + DT_RANK, :], ACT.Copy), [mm, last.get("x_dbl"), bc_sent.get(c - 1)]))
            bc_sent[c] = op("sync", "dma_bc", lambda e: e.dma_start(bc_dram[c], x_dbl[0:BC, :]), [cp])
            yield
            for h in range(HALVES):
                g, free = work(FRONT)
                mm = op("tensor", "dt_proj", lambda e, h=h, g=g: e.matmul(
                    work_bank[g][:], w_dt[dt_rows, h * P:(h + 1) * P], x_dbl[dt_rows, :], start=True, stop=True), [cp, free])
                yield
                t = op("scalar", "pre_dt", lambda e, h=h, g=g: e.activation(
                    delta[:, s2, h, :], work_bank[g][:], ACT.Identity, bias=b_dt[:, h:h + 1]), [mm, d_read.get(c - 2)])
                release(g, t)
            last["x_dbl"] = mm
            yield
            t = op("scalar", "abs_dt", lambda e: e.activation(exp_dt[:], delta[:, s2], ACT.Abs), [t])
            z = op("scalar", "exp_dt", lambda e: e.activation(exp_dt[:], exp_dt[:], ACT.Exp, scale=-1.0), [t])
            yield
            ln = op("scalar", "log_dt", lambda e: e.activation(du[:, s2], exp_dt[:], ACT.Ln, bias=1.0), [z, du_read.get(c - 2)])
            t = op("vector", "series", lambda e: e.tensor_scalar(ser_dt[:], exp_dt[:], -0.25, 1.0 / 3.0, ALU.mult, ALU.add), [z])
            for k in (0.0, -0.5, 1.0):
                t = op("vector", "series", lambda e, k=k: e.scalar_tensor_tensor(
                    ser_dt[:], ser_dt[:], k, exp_dt[:], ALU.add, ALU.mult), [t])
            yield
            mk = op("vector", "small", lambda e: e.tensor_scalar(exp_dt[:].bitcast(u32), exp_dt[:], 2.0 ** -6, None, ALU.is_lt), [t, ln])
            t = op("vector", "log1p", lambda e: e.copy_predicated(du[:, s2], exp_dt[:].bitcast(u32), ser_dt[:]), [mk, ln])
            t = op("vector", "delta", lambda e: e.scalar_tensor_tensor(
                delta[:, s2], delta[:, s2], 0.0, du[:, s2], ALU.max, ALU.add), [t, d_read.get(c - 2)])
            last["pre_dt"] = last["conv"] = last["tanh_c"] = t
            t = op("vector", "du", lambda e: e.tensor_tensor(du[:, s2], delta[:, s2], xc[:, s2], ALU.mult), [t, du_read.get(c - 2)])
            scan_in_ready[c] = t
            yield
            zs = []
            for h in range(HALVES):
                g, free = work(FRONT)
                mm = op("tensor", "in_proj", lambda e, h=h, g=g: e.matmul(
                    work_bank[g][:], w_in[:, D_INNER + h * P:D_INNER + (h + 1) * P], u_t[:], start=True, stop=True), [free])
                yield
                th = op("scalar", "tanh_z", lambda e, g=g, h=h: e.activation(silu_z[:, s2, h, :], work_bank[g][:], ACT.Tanh), [mm, z_free.get(c - 2)])
                z = op("vector", "silu_z", lambda e, h=h, g=g: e.scalar_tensor_tensor(
                    silu_z[:, s2, h, :], silu_z[:, s2, h, :], 1.0, work_bank[g][:], ALU.add, ALU.mult), [th])
                release(g, z)
                zs.append(z)
            last["u_t"] = mm
            z_ready[c] = zs[-1]
            yield

        inflow_ready, b_fetched, c_fetched, scanned, multiplied, summed, carried = {}, {}, {}, {}, {}, {}, {}
        decayed = {}
        units = [(c, n) for c in range(CHUNKS) for n in range(D_STATE)]
        last_y_read = {}

        def fetch(wide, name, i, row, freed):
            c, n = units[i]
            return op("sync", f"dma_{name}{i % ROW_SLOTS}", lambda e: e.dma_start(
                wide[:, i % ROW_SLOTS, :], bc_dram[c][row:row + 1, :].to_broadcast([P, CHUNK])), [bc_sent[c], freed])

        def fetch_b(i):
            if i < len(units):
                b_fetched[i] = fetch(b_wide, "b", i, units[i][1], inflow_ready.get(i - ROW_SLOTS))

        def fetch_c(i):
            if i < len(units):
                c_fetched[i] = fetch(c_wide, "c", i, D_STATE + units[i][1], multiplied.get(i - ROW_SLOTS))

        def prepare(i):
            if i >= len(units):
                return
            c, n = units[i]
            inflow_ready[i] = du_read[c] = op("gpsimd", "inflow", lambda e: e.tensor_tensor(
                inflow[:, i % 3], du[:, c % 2], b_wide[:, i % ROW_SLOTS:i % ROW_SLOTS + 1, :].to_broadcast([P, HALVES, CHUNK]), ALU.mult),
                [b_fetched[i], scan_in_ready[c], scanned.get(i - 3)])

        def decay(i, h):
            if i >= len(units):
                return
            c, n = units[i]
            decayed[(i, h)] = d_read[c] = op("scalar", "decay", lambda e: e.activation(
                decay_bank[h][:], delta[:, c % 2, h, :], ACT.Exp, scale=a_neg[:, h, n:n + 1]),
                [scan_in_ready[c], a_ready, scanned.get((i - 1, h))])

        def scan(i, h):
            c, n = units[i]
            initial = 0.0 if c % (SEQ // CHUNK) == 0 else carry[:, n, h:h + 1]
            scanned[(i, h)] = scanned[i] = op("vector", "scanned", lambda e: e.tensor_tensor_scan(
                state[:, i % 2, h, :], decay_bank[h][:], inflow[:, i % 3, h, :], initial, ALU.mult, ALU.add),
                [decayed[(i, h)], inflow_ready[i], multiplied.get(i - 2), carried.get(i - 2), carried.get(i - D_STATE)])

        def times_c(i):
            c, n = units[i]
            carried[i] = op("gpsimd", "carried", lambda e: e.tensor_copy(carry[:, n, :], state[:, i % 2, :, CHUNK - 1]), [scanned[i]])
            multiplied[i] = op("vector", "times_c", lambda e: e.tensor_tensor(
                prod[:, i % 2], state[:, i % 2], c_wide[:, i % ROW_SLOTS:i % ROW_SLOTS + 1, :].to_broadcast([P, HALVES, CHUNK]), ALU.mult),
                [scanned[i], c_fetched[i], summed.get(i - 2)])

        def total(i):
            c, n = units[i]
            for h in range(HALVES):
                if n == 0:
                    xc_free[c] = op("tensor", "y_skip", lambda e, h=h: e.matmul(
                        y_bank[h][:], diag_d[:, h, :], xc[:, c % 2, h, :], start=True, stop=False),
                        [xc_ready[c], diag_ready, last_y_read.get((c - 1, h))])
                summed[i] = op("tensor", "y_sum", lambda e, h=h: e.matmul(
                    y_bank[h][:], ident[:], prod[:, i % 2, h, :], start=False, stop=n == D_STATE - 1), [multiplied[i]])
            if n == D_STATE - 1:
                y_done[c] = summed[i]

        def take_y(c):
            s2 = c % 2
            for h in range(HALVES):
                t = op("vector", "y_gate", lambda e, h=h: e.tensor_tensor(
                    y_gated[:, h, :], silu_z[:, s2, h, :], y_bank[h][:], ALU.mult), [y_done[c], z_ready[c], last.get("y_gated")])
                last_y_read[(c, h)] = t
            z_free[c] = last["y_gate"] = t

        x_four_ready, row_sent, experts_ready, slots_loaded, combined = {}, {}, {}, {}, {}
        gate_done, expert_reg, up_done, tanh_ready, h_turned, down_done, cols_made = {}, {}, {}, {}, {}, {}, {}

        def back(c):
            sx, s2 = c % 3, c % 2
            g, free = work(SIDE)
            for s in range(SUB):
                for h in range(HALVES):
                    mm = op("tensor", "out_proj", lambda e, s=s, h=h, g=g: e.matmul(
                        work_bank[g][:, s * P:(s + 1) * P], y_gated[:, h, s * P:(s + 1) * P], w_out[:, h, :],
                        start=h == 0, stop=h == HALVES - 1), [last["y_gate"], free, back_w])
            last["y_gated"] = mm
            yield
            t = op("vector", "x_two", lambda e, g=g: e.tensor_tensor(
                x_two[:], x_one[:, sx], work_bank[g][:].rearrange("p (s d) -> p s d", s=SUB), ALU.add), [mm, x_one_ready[c]])
            x_one_free[c] = release(g, t)
            x2 = t
            xb = op("gpsimd", "x_plus_b", lambda e: e.tensor_tensor(
                x_tok[:, c], x_tok[:, c], b_ffp[:].rearrange("p (o d) -> p o d", o=1).to_broadcast([P, SUB, D_MODEL]), ALU.add), [x_one_ready[c], back_w])
            yield
            yield from norm(x_two, n_tok, 2, [t], [last.get("n_tok")])
            t = last[("normed", 2)]
            g, t = transposes(SIDE, n_tok, [t])
            last["n_tok"] = t
            yield
            t = op("scalar", "n_t", lambda e, g=g: e.activation(n_t[:], work_bank[g][:], ACT.Identity,
                                                              bias=norm_gb[:, 3:4], scale=norm_gb[:, 2:3]), [t, last.get("n_t")])
            release(g, t)
            g, free = work(SIDE)
            mm = op("tensor", "ff_gate", lambda e, g=g: e.matmul(work_bank[g][:], w_ffg[:, 0:P], n_t[:], start=True, stop=True),
                    [t, free, back_ready[0]])
            yield
            th = op("scalar", "tanh_g", lambda e, g=g: e.activation(tanh_g[:], work_bank[g][:], ACT.Tanh, bias=b_ffg[:, 0:1]), [mm, last.get("gate_h")])
            t = op("scalar", "gate_h", lambda e, g=g: e.activation(gate_h[:], work_bank[g][:], ACT.Identity, bias=b_ffg[:, 0:1]), [mm, last.get("ff_h")])
            release(g, t)
            g, free = work(SIDE)
            mm = op("tensor", "ff_val", lambda e, g=g: e.matmul(work_bank[g][:], w_ffg[:, P:], n_t[:], start=True, stop=True), [free])
            last["n_t"] = mm
            yield
            t = op("vector", "silu_g", lambda e: e.scalar_tensor_tensor(gate_h[:], tanh_g[:], 1.0, gate_h[:], ALU.add, ALU.mult), [t, th])
            t = op("vector", "ff_h", lambda e, g=g: e.scalar_tensor_tensor(
                ff_h[:], work_bank[g][:], b_ffg[:, 1:2], gate_h[:], ALU.add, ALU.mult), [t, mm, last.get("ff_h")])
            last["gate_h"] = release(g, t)
            g, free = work(SIDE)
            for s in range(SUB):
                mm = op("tensor", "ff_out", lambda e, s=s, g=g: e.matmul(
                    work_bank[g][:, s * P:(s + 1) * P], ff_h[:, s * P:(s + 1) * P], w_ffp[:], start=True, stop=True), [t, free])
            last["ff_h"] = mm
            yield
            t = op("vector", "x_three", lambda e, g=g: e.tensor_tensor(
                x_two[:], x_two[:], work_bank[g][:].rearrange("p (s d) -> p s d", s=SUB), ALU.add), [mm])
            release(g, t)
            t = x_four_ready[c] = op("vector", "x_four", lambda e: e.tensor_tensor(x_tok[:, c], x_two[:], x_tok[:, c], ALU.add), [t, xb])
            yield
            yield from norm(x_tok[:, c], m_tok, 3, [t], [last.get("m_tok"), row_sent.get(c - 1)])
            t = last[("normed", 3)]
            group = next(k for k, cs in enumerate(GROUPS) if c in cs)
            at = c - GROUPS[group][0]
            row_sent[c] = op("sync", f"dma_rows{s2}", lambda e: e.dma_start(
                row_dram[group][at * CHUNK:(at + 1) * CHUNK].rearrange("(s p) d -> p s d", p=P), m_tok[:]), [t])
            g, t = transposes(SIDE, m_tok, [t])
            last["m_tok"] = t
            yield
            t = op("scalar", "m_t", lambda e, g=g: e.activation(m_t[:], work_bank[g][:], ACT.Copy), [t, last.get("m_t")])
            release(g, t)
            yield
            g, free = work(SIDE)
            for s in range(SUB):
                mm = op("tensor", "route", lambda e, s=s, g=g: e.matmul(
                    work_bank[g][:, s * EXPERTS:(s + 1) * EXPERTS], m_t[:, s * P:(s + 1) * P], w_route[:], start=True, stop=True), [t, free])
            last["m_t"] = mm
            yield
            t = op("vector", "logits", lambda e, g=g: e.tensor_tensor(
                logits[:], work_bank[g][:, :SUB * EXPERTS].rearrange("p (s e) -> p s e", s=SUB),
                b_route[:].rearrange("p (o e) -> p o e", o=1).to_broadcast([P, SUB, EXPERTS]), ALU.add), [mm, last.get("logits")])
            release(g, t)
            for s in range(SUB):
                mx = op("vector", "top", lambda e, s=s: e.max(top8[:, s, :], logits[:, s, :]), [t, last.get("top8")])
            for s in range(SUB):
                ix = op("vector", "top", lambda e, s=s: e.max_index(top_i[:, s, :], top8[:, s, :], logits[:, s, :]), [mx, last.get("logits")])
            gap = op("vector", "gap", lambda e: e.tensor_tensor(top_w[:, 0, :], top8[:, :, 1], top8[:, :, 0], ALU.subtract), [ix, last.get("top_w")])
            last["top8"] = gap
            t = last["logits"] = op("vector", "top", lambda e: e.tensor_copy(top_if[:], top_i[:]), [ix, last.get("choice")])
            ex = op("scalar", "route_exp", lambda e: e.activation(top_w[:, 0, :], top_w[:, 0, :], ACT.Exp), [gap])
            yield
            tiles = slice(c * SUB, (c + 1) * SUB)
            for k in range(TOPK):
                t2 = op("vector", "choice", lambda e, k=k: e.tensor_tensor(
                    choice[:, k, tiles, :], iota8[:].rearrange("p (o e) -> p o e", o=1).to_broadcast([P, SUB, EXPERTS]),
                    top_if[:, :, k:k + 1].to_broadcast([P, SUB, EXPERTS]), ALU.is_equal), [t])
            last["choice"] = t2
            chosen = op("vector", "both", lambda e: e.tensor_tensor(both[:], choice[:, 0, tiles, :], choice[:, 1, tiles, :], ALU.add), [t2, last.get("both")])
            t = op("vector", "weights", lambda e: e.tensor_scalar(top_w[:, 1, :], top_w[:, 0, :], 1.0, None, ALU.add), [ex])
            t = op("vector", "weights", lambda e: e.reciprocal(choice_w[:, 0, tiles], top_w[:, 1, :]), [t])
            t = last["top_w"] = op("vector", "weights", lambda e: e.tensor_tensor(choice_w[:, 1, tiles], top_w[:, 0, :], choice_w[:, 0, tiles], ALU.mult), [t])
            yield
            g, free = work(SIDE)
            op("tensor", "rank", lambda e, g=g: e.matmul(work_bank[g][:, 0:SUB * EXPERTS], before[:], both[:].rearrange("p s e -> p (s e)"),
                                                       start=True, stop=True), [chosen, free])
            mm = last["both"] = op("tensor", "rank", lambda e, g=g: e.matmul(
                work_bank[g][:, SUB * EXPERTS:2 * SUB * EXPERTS], ones[:], both[:].rearrange("p s e -> p (s e)"), start=True, stop=True), [ones_made])
            yield
            t = op("vector", "tile_sum", lambda e, g=g: e.tensor_copy(
                tile_sum[:].rearrange("p k s e -> p (k s e)"), work_bank[g][:, 0:2 * SUB * EXPERTS]), [mm, last.get("tile_sum")])
            release(g, t)
            if c == GROUPS[group][0]:
                t = op("vector", "count", lambda e: e.memset(count[:, 0, :], 0.0), [t, last.get("count")])
            for s in range(SUB):
                op("vector", "count", lambda e, s=s: e.tensor_tensor(
                    rank[:, c * SUB + s, :], tile_sum[:, 0, s, :], count[:, s % 2, :], ALU.add), [t, last.get("count")])
                t = last["count"] = op("vector", "count", lambda e, s=s: e.tensor_tensor(
                    count[:, 1 - s % 2, :], tile_sum[:, 1, s, :], count[:, s % 2, :], ALU.add), [t])
            last["tile_sum"] = t
            yield
            if c == GROUPS[group][-1]:
                yield from sort_pairs(group, t)

        def sort_pairs(k, counted):
            chunks, n_tiles = GROUPS[k], TILES[k]
            first, n_tok = chunks[0] * SUB, len(chunks) * SUB
            mine = slice(first, first + n_tok)
            t = op("vector", "sort", lambda e: e.tensor_scalar(tiles_i[:], count[:, 0, :], float(P - 1), None, ALU.add), [counted, last.get("sort")])
            t = op("vector", "sort", lambda e: e.tensor_single_scalar(tiles_i[:], tiles_i[:], 7, ALU.arith_shift_right), [t])
            t = op("vector", "sort", lambda e: e.tensor_copy(tiles_f[:], tiles_i[:]), [t])
            t = op("vector", "sort", lambda e: e.tensor_tensor_scan(tiles_end[:], ones[:, 0:EXPERTS], tiles_f[:], 0.0, ALU.mult, ALU.add), [t, ones_made])
            t = op("vector", "sort", lambda e: e.tensor_tensor(start[:], tiles_end[:], tiles_f[:], ALU.subtract), [t])
            t = op("vector", "sort", lambda e: e.tensor_scalar(start[:], start[:], float(P), None, ALU.mult), [t])
            t = op("vector", "sort", lambda e: e.tensor_tensor(
                passed[:, :n_tiles, :], iota_tile[:, :n_tiles].rearrange("p (j o) -> p j o", o=1).to_broadcast([P, n_tiles, EXPERTS]),
                tiles_end[:].rearrange("p (o e) -> p o e", o=1).to_broadcast([P, n_tiles, EXPERTS]), ALU.is_ge), [t])
            t = op("vector", "sort", lambda e: e.tensor_reduce(expert_f[:, :n_tiles], passed[:, :n_tiles, :], AX.X, ALU.add), [t])
            t = op("vector", "sort", lambda e: e.tensor_scalar(expert_i[:, k, :n_tiles], expert_f[:, :n_tiles], float(EXPERTS - 1), None, ALU.min), [t])
            experts_ready[k] = t
            yield
            t = op("vector", "sort", lambda e: e.tensor_tensor(
                rank[:, mine, :], rank[:, mine, :], start[:].rearrange("p (o e) -> p o e", o=1).to_broadcast([P, n_tok, EXPERTS]), ALU.add), [t])
            for q in range(TOPK):
                t = op("vector", "sort", lambda e, q=q: e.tensor_tensor(picked[:, mine, :], rank[:, mine, :], choice[:, q, mine, :], ALU.mult), [t])
                t = op("vector", "sort", lambda e: e.tensor_reduce(place_f[:, mine], picked[:, mine, :], AX.X, ALU.add), [t])
                t = op("vector", "sort", lambda e, q=q: e.tensor_copy(place[:, q, mine], place_f[:, mine]), [t])
                t = op("vector", "sort", lambda e, q=q: e.tensor_single_scalar(place_lo[:, mine], place[:, q, mine].bitcast(i32), P - 1, ALU.bitwise_and), [t])
                t = op("vector", "sort", lambda e, q=q: e.tensor_single_scalar(place_hi[:, mine], place[:, q, mine].bitcast(i32), 7, ALU.arith_shift_right), [t])
                t = op("vector", "sort", lambda e, q=q: e.tensor_copy(place_lf[:, q, mine], place_lo[:, mine]), [t])
                t = last["sort"] = op("vector", "sort", lambda e, q=q: e.tensor_copy(place_hf[:, q, mine], place_hi[:, mine]), [t])
            g, free = work(SIDE)
            mm, pairs = {}, [(tile, q) for tile in range(first, first + n_tok) for q in range(TOPK)]
            for m, (tile, q) in enumerate(pairs):
                lo = op("vector", "hot", lambda e, m=m, tile=tile, q=q: e.tensor_scalar(
                    hot_lo[:, m % 2, :], iota_p[:], place_lf[:, q, tile:tile + 1], None, ALU.is_equal), [t, mm.get(m - 2, last.get("hot"))])
                hi = op("vector", "hot", lambda e, m=m, tile=tile, q=q: e.tensor_scalar(
                    hot_hi[:, m % 2, :n_tiles], iota_tile[:, :n_tiles], place_hf[:, q, tile:tile + 1],
                    token_id[:, tile - first:tile - first + 1], ALU.is_equal, ALU.mult), [mm.get(m - 2)])
                mm[m] = op("tensor", "slot_sum", lambda e, m=m, g=g: e.matmul(
                    work_bank[g][:, :n_tiles], hot_lo[:, m % 2, :], hot_hi[:, m % 2, :n_tiles],
                    start=m == 0, stop=m == len(pairs) - 1), [hi, free])
                if m % 4 == 3:
                    yield
            last["hot"] = mm[len(pairs) - 1]
            yield
            slots_loaded[k] = release(g, op("vector", "slot_token", lambda e, g=g: e.tensor_copy(
                slot_token[:, k, :n_tiles], work_bank[g][:, :n_tiles]), [last["hot"]]))
            yield

        gathered, cols_ready, h_ready, g_free, y_sent = {}, {}, {}, {}, {}
        jobs = [(k, j) for k, n in enumerate(TILES) for j in range(n)]

        def gather(m):
            if m >= len(jobs) or m in gathered:
                return
            k, j = jobs[m]
            if k not in slots_loaded:
                return
            gathered[m] = op("gpsimd", f"dma_gather{m % 3}", lambda e: e.indirect_dma_start(
                x_rows[:, m % 3, :], None, row_dram[k], bass.IndirectOffsetOnAxis(slot_token[:, k, j:j + 1], 0)),
                [slots_loaded[k], row_sent[GROUPS[k][-1]], row_sent[GROUPS[k][-1] - 1], cols_ready.get(m - 3)])

        def turn_rows(m, banks):
            if m not in gathered or m in cols_ready:
                return
            mm = op("tensor", "x_turned", lambda e: e.transpose(banks[0][:, NF * P:NF * P + P], x_rows[:, m % 3, :], ident[:]), [gathered[m], g_free.get(id(banks[0]))])
            cols_ready[m] = g_free[id(banks[0])] = op("scalar", "x_cols", lambda e: e.activation(x_cols[:, m % 2, :], banks[0][:, NF * P:NF * P + P], ACT.Copy), [mm, up_done.get(m - 2)])

        def tile_up(m, banks):
            k, j = jobs[m]

            def gate(e):
                reg = e.value_load(expert_i[0:1, k, j:j + 1], min_val=0, max_val=EXPERTS - 1)
                expert_reg[m] = reg
                return e.matmul(banks[0][:, 0:FF], x_cols[:, m % 2, :], w_gate[:, bass.ds(reg, 1), :].rearrange("p o f -> p (o f)"), start=True, stop=True)

            gate_done[m] = op("tensor", "moe_gate", gate, [cols_ready[m], experts_ready[k], g_free.get(id(banks[0])), back_ready[0]])
            up_done[m] = op("tensor", "moe_up", lambda e: e.matmul(
                banks[1][:, 0:FF], x_cols[:, m % 2, :], w_up[:, bass.ds(expert_reg[m], 1), :].rearrange("p o f -> p (o f)"), start=True, stop=True), [g_free.get(id(banks[1]))])

        def tile_tanh(m, banks):
            tanh_ready[m] = op("scalar", "tanh_m", lambda e: e.activation(h_rows[:, m % 2, :], banks[0][:, 0:FF], ACT.Tanh), [gate_done[m], h_turned.get(m - 2)])

        def tile_h(m, banks):
            t = op("vector", "silu_m", lambda e: e.scalar_tensor_tensor(
                silu_m[:], h_rows[:, m % 2, :], 1.0, banks[0][:, 0:FF], ALU.add, ALU.mult), [tanh_ready[m], h_ready.get(m - 1)])
            h_ready[m] = g_free[id(banks[0])] = op("vector", "moe_h", lambda e: e.tensor_tensor(
                h_rows[:, m % 2, :], silu_m[:], banks[1][:, 0:FF], ALU.mult), [t, up_done[m]])
            g_free[id(banks[1])] = h_ready[m]

        def tile_turn(m, banks):
            for q, (f, n) in enumerate(F_TILES):
                mm = op("tensor", "h_turned", lambda e, q=q, f=f, n=n: e.transpose(
                    banks[0][:n, q * P:(q + 1) * P], h_rows[:, m % 2, f:f + n], ident[:]), [h_ready[m], g_free[id(banks[0])]])
            h_turned[m] = mm
            f, n = F_TILES[-1]
            full = NF - 1
            op("scalar", "h_cols", lambda e: e.activation(
                h_cols[:, m % 2, 0:full, :], banks[0][:, 0:full * P].rearrange("p (q t) -> p q t", q=full), ACT.Copy), [mm, down_done.get(m - 2)])
            t = g_free[id(banks[0])] = op("scalar", "h_cols", lambda e: e.activation(
                h_cols[:n, m % 2, full, :], banks[0][:n, full * P:NF * P], ACT.Copy))
            cols_made[m] = t

        def tile_down(m, banks):
            k, j = jobs[m]
            t = cols_made[m]
            for q, (f, n) in enumerate(F_TILES):
                mm = op("tensor", "moe_down", lambda e, q=q, n=n: e.matmul(
                    banks[1][:, 0:D_MODEL], h_cols[:n, m % 2, q, :], w_down[:n, bass.ds(expert_reg[m], 1), q, :].rearrange("p o d -> p (o d)"),
                    start=q == 0, stop=q == NF - 1), [t, g_free[id(banks[1])]])
            down_done[m] = mm
            t = g_free[id(banks[1])] = op("scalar", "y_rows", lambda e: e.activation(y_rows[:, m % 2, :], banks[1][:, 0:D_MODEL], ACT.Copy), [mm, y_sent.get(m - 2)])
            y_sent[m] = op("sync", f"dma_y{m % 2}", lambda e: e.dma_start(y_dram[k][j * P:(j + 1) * P, :], y_rows[:, m % 2, :]), [t])

        def combine(k):
            ends = [y_sent[m] for m in range(len(jobs)) if jobs[m][0] == k][-2:]
            for c in GROUPS[k]:
                for s in range(SUB):
                    tile = c * SUB + s
                    got = []
                    for q in range(TOPK):
                        got.append(op("gpsimd", f"dma_pair{tile % 2}", lambda e, q=q, tile=tile: e.indirect_dma_start(
                            y_pair[:, tile % 2, q, :], None, y_dram[k], bass.IndirectOffsetOnAxis(place[:, q, tile:tile + 1], 0)),
                            ends + [combined.get(tile - 2), combined.get(("order", k))]))
                    if s % 2:
                        yield
                    for q in range(TOPK):
                        t = op("vector", "combined", lambda e, q=q, s=s, c=c, tile=tile: e.scalar_tensor_tensor(
                            x_tok[:, c, s, :], y_pair[:, tile % 2, q, :], choice_w[:, q, tile:tile + 1], x_tok[:, c, s, :], ALU.mult, ALU.add),
                            [got[-1], x_four_ready[c], combined.get(tile) if q else None])
                        combined[tile] = t
                out_sent[c] = op("sync", "dma_out", lambda e, c=c: e.dma_start(out_dram[c], x_tok[:, c]), [t])
                yield

        for _ in front(0):
            pass
        halve_back()
        for i in range(ROW_SLOTS):
            fetch_b(i)
        for i in range(2):
            fetch_c(i)
            prepare(i)
        fetch_b(ROW_SLOTS)
        for h in range(HALVES):
            decay(0, h)
        sides, combining = [], []
        m = 0

        def step(gens, n=1):
            for _ in range(n):
                while gens and next(gens[0], "over") == "over":
                    gens.pop(0)

        def after_tile(m):
            k, j = jobs[m]
            if j == TILES[k] - 1:
                combining.append(combine(k))

        fronts = []
        for i in range(len(units)):
            c, n = units[i]
            if n == 0 and c + 1 < CHUNKS:
                fronts.append(front(c + 1))
            if n == D_STATE - 4:
                while c + 1 < CHUNKS and c + 1 not in bc_sent:
                    step(fronts)
            if n == D_STATE - 2:
                while c + 1 < CHUNKS and c + 1 not in scan_in_ready:
                    step(fronts)
            fetch_b(i + 4)
            fetch_c(i + 2)
            prepare(i + 2)
            moving = m < len(jobs) and m in cols_ready
            if not moving and m < len(jobs) and jobs[m][0] in slots_loaded:
                gather(m), gather(m + 1), gather(m + 2)
                turn_rows(m, expert_bank)
            if moving:
                tile_up(m, expert_bank)
            scan(i, 0)
            decay(i + 1, 0)
            scan(i, 1)
            if moving:
                tile_tanh(m, expert_bank)
            decay(i + 1, 1)
            if moving:
                tile_h(m, expert_bank)
            if i:
                total(i - 1)
            if n == 0 and c:
                take_y(c - 1)
                sides.append(back(c - 1))
            step(fronts)
            times_c(i)
            if moving:
                tile_turn(m, expert_bank)
                turn_rows(m + 1, expert_bank)
            step(sides)
            step(fronts)
            if moving:
                tile_down(m, expert_bank)
                gather(m + 3)
                after_tile(m)
                m += 1
            step(sides)
            step(combining)
        total(len(units) - 1)
        take_y(CHUNKS - 1)
        sides.append(back(CHUNKS - 1))
        step(sides, 999)
        pairs = [expert_bank, decay_bank, y_bank]
        for b in decay_bank:
            g_free[id(b)] = scanned[len(units) - 1]
        for h, b in enumerate(y_bank):
            g_free[id(b)] = last_y_read[(CHUNKS - 1, h)]
        rest = list(range(m, len(jobs)))
        for q in rest[:3]:
            gather(q)
        turn_rows(rest[0], pairs[rest[0] % 3])
        for q in rest + [len(jobs), len(jobs) + 1]:
            if q < len(jobs):
                tile_up(q, pairs[q % 3])
            if q + 1 < len(jobs):
                turn_rows(q + 1, pairs[(q + 1) % 3])
            if q < len(jobs):
                tile_tanh(q, pairs[q % 3])
            if rest[0] < q <= len(jobs):
                tile_turn(q - 1, pairs[(q - 1) % 3])
            if q < len(jobs):
                tile_h(q, pairs[q % 3])
            if q >= rest[0] + 2:
                tile_down(q - 2, pairs[(q - 2) % 3])
                after_tile(q - 2)
            gather(q + 3)
            step(combining)
        step(combining, 999)
        pr.wait("sync", [("dma_out", 16 * CHUNKS)] + [y_sent[q] for q in range(len(jobs) - 2, len(jobs))] + [row_sent[CHUNKS - 1], row_sent[CHUNKS - 2], bc_sent[CHUNKS - 1]])

        block = ctx.enter_context(nc.Block())

        @block.sync
        def _(eng):
            pr.play("sync", eng)

        @block.gpsimd
        def _(eng):
            pr.play("gpsimd", eng)

        @block.scalar
        def _(eng):
            pr.play("scalar", eng)

        @block.vector
        def _(eng):
            pr.play("vector", eng)

        @block.tensor
        def _(eng):
            pr.play("tensor", eng)


def shape_constants():
    ident = np.eye(P, dtype=np.float32)
    iota8 = np.tile(np.arange(EXPERTS, dtype=np.float32), (P, 1))
    iota_tile = np.tile(np.arange(max(TILES), dtype=np.float32), (P, 1))
    before = np.triu(np.ones((P, P), np.float32), 1)
    token_id = np.arange(TOKENS, dtype=np.float32).reshape(-1, P).T
    return {"ident": ident, "iota8": iota8,
            "iota_tile": iota_tile, "iota_p": np.tile(np.arange(P, dtype=np.float32), (P, 1)), "before": before, "token_id": token_id}


def columns(vector):
    return vector.reshape(-1, P).T


def kernel(**inputs):
    import concourse.bacc as bacc
    from concourse.bass_utils import run_bass_kernel_spmd as run

    a = {k.replace("L0_attn_", "").replace("L0_ffn_", ""): np.asarray(v) for k, v in inputs.items()}
    xproj = a["x_proj_w"]
    dt_rows, bc_rows = xproj[:DT_RANK], xproj[DT_RANK:]
    arrays = {
        "x": a["x"], **shape_constants(),
        "in_wT": a["in_proj_w"].T, "norm_gb": np.stack([a["n1_g"], a["n1_b"], a["n2_g"], a["n2_b"]], 1),
        "conv_w": a["conv_w"], "conv_b": columns(a["conv_b"]),
        "xproj_wT": np.concatenate([bc_rows, dt_rows], 0).T,
        "dt_wT": a["dt_w"].T, "dt_b": columns(a["dt_b"]), "A_log": a["A_log"], "D": columns(a["D"]), "out_wT": a["out_w"].T,
        "ffg_wT": a["ffg_w"].T, "ffg_b": columns(a["ffg_b"]), "ffp_wT": a["ffp_w"].T, "ffp_b": a["ffp_b"],
        "Ws": a["Ws"], "bs": a["bs"], "Wg": a["Wg"], "Wu": a["Wu"], "Wd": a["Wd"],
    }
    nc = bacc.Bacc("TRN2", target_bir_lowering=False, num_devices=1)
    feeds, T = {}, {}
    for name, array in arrays.items():
        array = np.ascontiguousarray(array)
        feeds[f"in_{name}"] = array
        T[name] = nc.dram_tensor(f"in_{name}", array.shape, mybir.dt.from_np(array.dtype), kind="ExternalInput").ap()
    out = nc.dram_tensor("out_0", (BATCH, SEQ, D_MODEL), mybir.dt.float32, kind="ExternalOutput").ap()
    mamba_moe_block(nc, T, out)
    result = run(nc, [feeds], core_ids=[0])
    return result.results[0]["out_0"]
```

```python
from contextlib import ExitStack

import numpy as np

import concourse.bass as bass
from concourse import mybir

BATCH, SEQ, D_MODEL = 2, 2048, 128
TOKENS = BATCH * SEQ
D_INNER, D_STATE, D_CONV, DT_RANK = 256, 16, 4, 8
HALVES = D_INNER // 128
EXPERTS, FF = 8, 344
EPS = 1e-5
P = 128
CHUNK = 512
SUB = CHUNK // P
CHUNKS = TOKENS // CHUNK
TOPK = 2
GROUPS = [range(0, 3), range(3, 5), range(5, 7), range(7, 8)]
TILES = [(TOPK * CHUNK * len(g) - EXPERTS) // P + EXPERTS for g in GROUPS]
HALO = D_CONV - 1
BC = 2 * D_STATE
HEAD_STEPS = 7
B_FROM = 3
MOST_TOK = SUB * max(len(g) for g in GROUPS)
STATE_SLOTS = 3
ROW_SLOTS = 3
F_TILES = [(f, min(P, FF - f)) for f in range(0, FF, P)]
NF = len(F_TILES)
FRONT, SIDE = 0, 1


class Program:

    def __init__(self, nc, ctx):
        self.nc, self.ctx = nc, ctx
        self.queue = {e: [] for e in ("sync", "gpsimd", "scalar", "vector", "tensor")}
        self.sems, self.count, self.seen = {}, {}, {}

    def op(self, engine, done, build, after=()):
        step = 16 if done.startswith("dma_") else 1
        if done not in self.sems:
            self.sems[done] = self.ctx.enter_context(self.nc.semaphore(done))
            self.count[done] = 0
        waits = []
        for token in after:
            if token is None:
                continue
            name, value = token
            if self.seen.get((engine, name), 0) < value:
                self.seen[(engine, name)] = value
                waits.append((self.sems[name], value))
        self.count[done] += step
        self.queue[engine].append((waits, build, self.sems[done], step))
        return (done, self.count[done])

    def wait(self, engine, after):
        waits = [(self.sems[n], v) for n, v in after]
        self.queue[engine].append((waits, None, None, 0))

    def play(self, engine, eng):
        for waits, build, sem, step in self.queue[engine]:
            for s, v in waits:
                eng.wait_ge(s, v)
            if build is not None:
                build(eng).then_inc(sem, step)


def mamba_moe_block(nc, T, out):
    f32, u32, i32 = mybir.dt.float32, mybir.dt.uint32, mybir.dt.int32
    ALU, ACT, AX = mybir.AluOpType, mybir.ActivationFunctionType, mybir.AxisListType
    ctx = ExitStack()
    with ctx:
        def sb(name, shape, dt=f32):
            return ctx.enter_context(nc.sbuf_tensor(name, shape, dt))

        def bank(name):
            return ctx.enter_context(nc.psum_tensor(name, [P, CHUNK], f32))

        pr = Program(nc, ctx)

        ident = sb("ident", [P, P])
        iota8 = sb("iota8", [P, EXPERTS])
        iota_tile = sb("iota_tile", [P, max(TILES)])
        before = sb("before", [P, P])
        ones = sb("ones", [P, P])
        token_id = sb("token_id", [P, TOKENS // P])
        iota_p = sb("iota_p", [P, P])
        w_in = sb("w_in", [P, 2 * D_INNER])
        w_conv = sb("w_conv", [P, HALVES, D_CONV])
        b_conv = sb("b_conv", [P, HALVES])
        w_xproj = sb("w_xproj", [P, HALVES, BC + DT_RANK])
        w_dt = sb("w_dt", [P, D_INNER])
        b_dt = sb("b_dt", [P, HALVES])
        a_neg = sb("a_neg", [P, HALVES, D_STATE])
        skip_d = sb("skip_d", [P, HALVES])
        diag_d = sb("diag_d", [P, HALVES, P])
        w_out = sb("w_out", [P, HALVES, D_MODEL])
        norm_gb = sb("norm_gb", [P, 4])
        w_ffg = sb("w_ffg", [P, 2 * D_MODEL])
        b_ffg = sb("b_ffg", [P, 2])
        w_ffp = sb("w_ffp", [P, D_MODEL])
        b_ffp = sb("b_ffp", [P, D_MODEL])
        w_route = sb("w_route", [P, EXPERTS])
        b_route = sb("b_route", [P, EXPERTS])
        w_gate = sb("w_gate", [P, EXPERTS, FF])
        w_up = sb("w_up", [P, EXPERTS, FF])
        w_down = sb("w_down", [P, EXPERTS, NF, D_MODEL])

        x_tok = sb("x_tok", [P, CHUNKS, SUB, D_MODEL])
        x_one = sb("x_one", [P, 3, SUB, D_MODEL])
        u_tok = sb("u_tok", [P, SUB, D_MODEL])
        u_t = sb("u_t", [P, 2, CHUNK])
        x_in = sb("x_in", [P, 2, HALVES, HALO + CHUNK])
        conv = sb("conv", [P, HALVES, CHUNK])
        tanh_c = sb("tanh_c", [P, HALVES, CHUNK])
        xc = sb("xc", [P, 2, HALVES, CHUNK])
        silu_z = sb("silu_z", [P, 2, HALVES, CHUNK])
        x_dbl = sb("x_dbl", [BC + DT_RANK, CHUNK])
        exp_dt, ser_dt = tanh_c, conv
        delta = sb("delta", [P, 2, HALVES, CHUNK])
        du = sb("du", [P, 2, HALVES, CHUNK])
        b_wide = sb("b_wide", [P, ROW_SLOTS, CHUNK])
        c_wide = sb("c_wide", [P, ROW_SLOTS, CHUNK])
        inflow = sb("inflow", [P, 3, HALVES, CHUNK])
        decayed_by = sb("decayed_by", [P, 2, HALVES, CHUNK])
        state = sb("state", [P, STATE_SLOTS, HALVES, CHUNK])
        carry = sb("carry", [P, D_STATE, HALVES])
        y_gated = sb("y_gated", [P, HALVES, CHUNK])
        x_two = sb("x_two", [P, SUB, D_MODEL])
        n_t = sb("n_t", [P, CHUNK])
        tanh_g = sb("tanh_g", [P, CHUNK])
        gate_h = sb("gate_h", [P, CHUNK])
        ff_h = gate_h
        m_tok = sb("m_tok", [P, SUB, D_MODEL])
        n_tok, m_t = m_tok, n_t
        logits = sb("logits", [P, SUB, EXPERTS])
        top8 = sb("top8", [P, SUB, 8])
        top_i = sb("top_i", [P, SUB, 8], u32)
        top_if = sb("top_if", [P, SUB, 8])
        top_w = sb("top_w", [P, 2, SUB])
        both = sb("both", [P, SUB, EXPERTS])
        tile_sum = sb("tile_sum", [P, 2, SUB, EXPERTS])
        choice_w = sb("choice_w", [P, TOPK, TOKENS // P])
        choice = sb("choice", [P, TOPK, TOKENS // P, EXPERTS])
        rank = sb("rank", [P, TOKENS // P, EXPERTS])
        count = sb("count", [P, 2, EXPERTS])
        tiles_i = sb("tiles_i", [P, EXPERTS], i32)
        tiles_f = sb("tiles_f", [P, EXPERTS])
        tiles_end = sb("tiles_end", [P, EXPERTS])
        start = sb("start", [P, EXPERTS])
        passed = sb("passed", [P, max(TILES), EXPERTS])
        expert_f = sb("expert_f", [P, max(TILES)])
        expert_i = sb("expert_i", [P, len(GROUPS), max(TILES)], i32)
        picked = sb("picked", [P, TOPK, MOST_TOK, EXPERTS])
        place_f = sb("place_f", [P, TOPK, MOST_TOK])
        place = sb("place", [P, TOPK, TOKENS // P], u32)
        place_hi = sb("place_hi", [P, TOPK, MOST_TOK], i32)
        place_lf = sb("place_lf", [P, TOPK, MOST_TOK])
        place_hf = sb("place_hf", [P, TOPK, MOST_TOK])
        hot_lo = sb("hot_lo", [P, SUB, P])
        hot_hi = sb("hot_hi", [P, SUB, max(TILES)])
        slot_token = sb("slot_token", [P, len(GROUPS), max(TILES)], u32)
        x_rows = sb("x_rows", [P, 3, D_MODEL])
        x_cols = sb("x_cols", [P, 2, P])
        silu_m = sb("silu_m", [P, FF])
        h_rows = sb("h_rows", [P, 2, FF])
        h_cols = sb("h_cols", [P, 2, NF, P])
        y_rows = sb("y_rows", [P, 2, D_MODEL])
        y_pair = sb("y_pair", [P, 2, TOPK, D_MODEL])
        var_one = sb("var_one", [P, SUB])
        stats = sb("stats", [P, SUB, 6])
        mean_var = sb("mean_var", [P, 4, SUB, 2])
        rstd = sb("rstd", [P, 4, SUB])
        shift = sb("shift", [P, 4, SUB])
        minus_half = sb("minus_half", [P, SUB])

        y_bank = [bank("y0"), bank("y1")]
        work_bank = [bank("work_front"), bank("work_side")]
        expert_banks = [[bank("gate0"), bank("up0")], [bank("gate1"), bank("up1")]]
        work_free, held = [None, None], set()

        def work(g):
            assert g not in held
            held.add(g)
            return g, work_free[g]

        def release(g, token):
            held.discard(g)
            work_free[g] = token
            return token

        op = pr.op

        def load(dst, src, name="dma_weights", engine="sync", after=()):
            return op(engine, name, lambda e: e.dma_start(dst, src), after)

        x_dram = T["x"].rearrange("b (c s p) d -> (b c) p s d", s=SUB, p=P)
        out_dram = out.rearrange("b (c s p) d -> (b c) p s d", s=SUB, p=P)
        x_loaded, out_sent = {}, {}

        def load_x(c, after=()):
            x_loaded[c] = load(x_tok[:, c], x_dram[c], f"dma_x{c}", after=after)

        load_x(0)
        load(ident[:], T["ident"])
        load(w_in[:], T["in_wT"])
        load(norm_gb[:], T["norm_gb"])
        load(w_conv[:], T["conv_w"].rearrange("(h p) o k -> p h (o k)", p=P))
        load(b_conv[:], T["conv_b"])
        load(w_xproj[:], T["xproj_wT"].rearrange("(h p) m -> p h m", p=P))
        load(w_dt[BC:BC + DT_RANK, :], T["dt_wT"])
        load(b_dt[:], T["dt_b"])
        load(a_neg[:], T["A_log"].rearrange("(h p) n -> p h n", p=P))
        front_w = load(skip_d[:], T["D"])
        load_x(1)
        for dst, src in ((w_out[:], T["out_wT"].rearrange("(h p) m -> p h m", p=P)), (w_ffg[:], T["ffg_wT"]),
                         (b_ffg[:], T["ffg_b"]), (w_ffp[:], T["ffp_wT"]),
                         (b_ffp[:], T["ffp_b"].rearrange("(o d) -> o d", o=1).to_broadcast([P, D_MODEL])),
                         (w_route[:], T["Ws"]), (iota8[:], T["iota8"]), (iota_tile[:], T["iota_tile"]), (before[:], T["before"]),
                         (token_id[:], T["token_id"]), (iota_p[:], T["iota_p"]),
                         (b_route[:], T["bs"].rearrange("(o d) -> o d", o=1).to_broadcast([P, EXPERTS])),
                         (w_gate[:], T["Wg"].rearrange("e d f -> d e f")), (w_up[:], T["Wu"].rearrange("e d f -> d e f"))):
            back_w = load(dst, src, "dma_back_weights")
        for j, (f, n) in enumerate(F_TILES):
            back_w = load(w_down[:n, :, j, :], T["Wd"][:, f:f + n, :].rearrange("e f d -> f e d"), "dma_back_weights")
        for c in range(2, CHUNKS):
            load_x(c)
        bc_dram = [nc.dram_tensor(f"bc_dram{c}", (BC, CHUNK), f32, kind="Internal").ap() for c in range(CHUNKS)]
        row_dram = [nc.dram_tensor(f"row_dram{k}", (CHUNK * len(g), D_MODEL), f32, kind="Internal").ap() for k, g in enumerate(GROUPS)]
        y_dram = [nc.dram_tensor(f"y_dram{k}", (P * n, D_MODEL), f32, kind="Internal").ap() for k, n in enumerate(TILES)]

        op("vector", "halved", lambda e: e.tensor_scalar(w_in[:, D_INNER:], w_in[:, D_INNER:], 0.5, None, ALU.mult), [front_w])
        op("vector", "halved", lambda e: e.tensor_scalar(w_conv[:], w_conv[:], 0.5, None, ALU.mult))
        front_ready = op("vector", "halved", lambda e: e.tensor_scalar(b_conv[:], b_conv[:], 0.5, None, ALU.mult))
        a_exp = op("scalar", "a_exp", lambda e: e.activation(a_neg[:], a_neg[:], ACT.Exp), [front_w])
        a_ready = op("vector", "a_ready", lambda e: e.tensor_scalar(a_neg[:], a_neg[:], -1.0, None, ALU.mult), [a_exp])
        for h in range(HALVES):
            diag_ready = op("vector", "diag_d", lambda e, h=h: e.tensor_scalar(diag_d[:, h, :], ident[:], skip_d[:, h:h + 1], None, ALU.mult), [front_w])
        half_made = op("gpsimd", "half_made", lambda e: e.memset(minus_half[:], -0.5))
        ones_made = op("gpsimd", "ones_made", lambda e: e.memset(ones[:], 1.0))
        zero0 = op("vector", "halo_zero", lambda e: e.memset(x_in[:, 0, :, 0:HALO], 0.0))
        back_ready = {}

        def halve_back():
            op("gpsimd", "back_halved", lambda e: e.tensor_scalar(w_ffg[:, :D_MODEL], w_ffg[:, :D_MODEL], 0.5, None, ALU.mult), [back_w])
            op("gpsimd", "back_halved", lambda e: e.tensor_scalar(b_ffg[:, 0:1], b_ffg[:, 0:1], 0.5, None, ALU.mult))
            back_ready[0] = op("gpsimd", "back_halved", lambda e: e.tensor_scalar(w_gate[:], w_gate[:], 0.5, None, ALU.mult))

        last = {}

        def prior(tokens, c):
            return tokens[c] if c >= 0 else None

        def until(queued):
            while not queued():
                yield

        def take(g):
            yield from until(lambda: g not in held)
            return work(g)

        def norm(src, dst, slot, after, free, chunk=None):
            for s in range(SUB):
                st = op("vector", "stats", lambda e, s=s: e.bn_stats(stats[:, s, :], src[:, s, :]), list(after) + [last.get("aggr")])
            for s in range(SUB):
                ag = last["aggr"] = op("vector", "aggr", lambda e, s=s: e.bn_aggr(mean_var[:, slot, s, :], stats[:, s, :]), [st, last.get(("normed", slot)), last.get("u_tok_made") if slot == 0 else None])
            yield
            t = rsqrt(slot, mean_var[:, slot, :, 1], [ag])
            if slot == 0:
                yield from second_rstd(t)
            yield
            t = op("vector", "shift", lambda e: e.scalar_tensor_tensor(
                shift[:, slot, :], mean_var[:, slot, :, 0], -1.0, rstd[:, slot, :], ALU.mult, ALU.mult), [t])
            yield
            if slot == 0:
                yield from until(lambda: chunk < 3 or chunk - 3 in x_one_free)
                free = [prior(x_one_free, chunk - 3)]
            for s in range(SUB):
                last[("normed", slot)] = op("scalar", "normed", lambda e, s=s: e.activation(
                    dst[:, s, :], src[:, s, :], ACT.Identity, bias=shift[:, slot, s:s + 1], scale=rstd[:, slot, s:s + 1]), [t] + list(free))

        def rsqrt(slot, var, after):
            t = op("gpsimd", "rstd", lambda e: e.tensor_scalar(rstd[:, slot, :], var, EPS, None, ALU.add), after)
            return op("gpsimd", "rstd", lambda e: e.tensor_tensor(rstd[:, slot, :], rstd[:, slot, :], minus_half[:], ALU.pow), [t, half_made])

        def second_rstd(t):
            v = op("gpsimd", "var_one", lambda e: e.tensor_tensor(var_one[:], mean_var[:, 0, :, 1], rstd[:, 0, :], ALU.mult), [t, last.get("u_tok_made")])
            v = op("gpsimd", "var_one", lambda e: e.tensor_tensor(var_one[:], var_one[:], rstd[:, 0, :], ALU.mult), [v])
            last["rstd_one"] = rsqrt(1, var_one[:], [v])
            yield

        def transposes(g, src, after):
            g, free = work(g)
            for s in range(SUB):
                tok = op("tensor", "transposed", lambda e, s=s, g=g: e.transpose(
                    work_bank[g][:, s * P:(s + 1) * P], src[:, s, :], ident[:]), list(after) + [free])
            return g, tok

        now = [-1]
        x_one_ready, u_made, xc_ready, dbl_ready, delta_ready, z_made, z_ready, scan_in_ready, bc_sent = {}, {}, {}, {}, {}, {}, {}, {}, {}
        y_done, d_read, du_read, xin_done = {}, {}, {}, {}
        xc_free, z_free, x_one_free, x_free = {}, {}, {}, {}

        def front_a(c):
            sx, s2 = c % 3, c % 2
            yield from norm(x_tok[:, c], x_one[:, sx], 0, [x_loaded[c]], [], chunk=c)
            t = x_one_ready[c] = last[("normed", 0)]
            for s in range(SUB):
                last["u_tok_made"] = op("scalar", "u_tok", lambda e, s=s: e.activation(
                    u_tok[:, s, :], x_one[:, sx, s, :], ACT.Copy, scale=rstd[:, 1, s:s + 1]), [t, last["rstd_one"], last.get("u_tok")])
            t = last["u_tok_made"]
            yield
            yield from until(lambda: FRONT not in held)
            g, t = transposes(FRONT, u_tok, [t, front_w])
            last["u_tok"] = t
            yield
            u_ready = release(g, op("scalar", "u_t", lambda e, g=g: e.activation(u_t[:, s2, :], work_bank[g][:], ACT.Identity,
                                                          bias=norm_gb[:, 1:2], scale=norm_gb[:, 0:1]), [t, prior(z_made, c - 2), front_w]))
            yield
            u_made[c] = u_ready
            cps = []
            for h in range(HALVES):
                g, free = yield from take(FRONT)
                mm = op("tensor", "in_proj", lambda e, h=h, g=g: e.matmul(
                    work_bank[g][:], w_in[:, h * P:(h + 1) * P], u_t[:, s2, :], start=True, stop=True), [u_ready, free, front_ready])
                yield
                cps.append(release(g, op("scalar", "x_in", lambda e, h=h, g=g: e.activation(
                    x_in[:, s2, h, HALO:], work_bank[g][:], ACT.Copy), [mm, prior(xin_done, c - 2)])))
                yield
            if c % (SEQ // CHUNK) == 0:
                halo = zero0 if c == 0 else op("vector", "halo_zero", lambda e: e.memset(x_in[:, s2, :, 0:HALO], 0.0), [xin_done[c - 2]])
            else:
                halo = op("vector", "halo", lambda e: e.tensor_copy(x_in[:, s2, :, 0:HALO], x_in[:, 1 - s2, :, CHUNK:]), [last["x_in"], prior(xin_done, c - 2)])
            last["x_in"] = cps[-1]
            yield
            yield from until(lambda: c == 0 or c - 1 in delta_ready)
            tap0 = []
            for h in range(HALVES):
                tap0.append(op("scalar", "conv0", lambda e, h=h: e.activation(
                    conv[:, h, :], x_in[:, s2, h, 0:CHUNK], ACT.Identity, bias=b_conv[:, h:h + 1], scale=w_conv[:, h, 0:1]),
                    [halo, cps[h], last.get("conv"), front_ready]))
            yield
            for h in range(HALVES):
                t = tap0[h]
                for k in range(1, D_CONV):
                    t = op("vector", "conv", lambda e, h=h, k=k: e.scalar_tensor_tensor(
                        conv[:, h, :], x_in[:, s2, h, k:k + CHUNK], w_conv[:, h, k:k + 1], conv[:, h, :], ALU.mult, ALU.add), [t])
                    yield
            xin_done[c] = t
            th = op("scalar", "tanh_c", lambda e: e.activation(tanh_c[:], conv[:], ACT.Tanh), [t, last.get("tanh_c")])
            yield
            t = op("vector", "xc", lambda e: e.scalar_tensor_tensor(
                xc[:, s2], tanh_c[:], 1.0, conv[:], ALU.add, ALU.mult), [th, prior(xc_free, c - 2)])
            xc_ready[c] = t
            yield
            g, free = yield from take(FRONT)
            for h in range(HALVES):
                mm = op("tensor", "x_proj", lambda e, h=h, g=g: e.matmul(
                    work_bank[g][0:BC + DT_RANK, :], w_xproj[:, h, :], xc[:, s2, h, :],
                    start=h == 0, stop=h == HALVES - 1), [t, free])
            yield
            dbl_ready[c] = cp = release(g, op("scalar", "x_dbl", lambda e, g=g: e.activation(
                x_dbl[:], work_bank[g][0:BC + DT_RANK, :], ACT.Copy), [mm, last.get("x_dbl"), prior(bc_sent, c - 1)]))
            bc_sent[c] = op("sync", "dma_bc", lambda e: e.dma_start(bc_dram[c], x_dbl[0:BC, :]), [cp])
            yield

        dt_rows = slice(BC, BC + DT_RANK)

        def front_b(c):
            s2 = c % 2
            yield from until(lambda: c in dbl_ready and (c == 0 or now[0] >= (c - 1) * D_STATE + B_FROM))
            for h in range(HALVES):
                g, free = yield from take(FRONT)
                mm = op("tensor", "dt_proj", lambda e, h=h, g=g: e.matmul(
                    work_bank[g][:], w_dt[dt_rows, h * P:(h + 1) * P], x_dbl[dt_rows, :], start=True, stop=True), [dbl_ready[c], free])
                yield
                t = op("scalar", "pre_dt", lambda e, h=h, g=g: e.activation(
                    delta[:, s2, h, :], work_bank[g][:], ACT.Identity, bias=b_dt[:, h:h + 1]), [mm, prior(d_read, c - 2)])
                release(g, t)
                yield
            last["x_dbl"] = mm
            t = op("scalar", "abs_dt", lambda e: e.activation(exp_dt[:], delta[:, s2], ACT.Abs), [t])
            z = op("scalar", "exp_dt", lambda e: e.activation(exp_dt[:], exp_dt[:], ACT.Exp, scale=-1.0), [t])
            yield
            t = op("scalar", "series", lambda e: e.activation(ser_dt[:], exp_dt[:], ACT.Copy, bias=1.0 / 3.0, scale=-0.25), [z])
            ln = op("scalar", "log_dt", lambda e: e.activation(du[:, s2], exp_dt[:], ACT.Ln, bias=1.0), [z, prior(du_read, c - 2)])
            yield
            for k in (0.0, -0.5, 1.0):
                t = op("vector", "series", lambda e, k=k: e.scalar_tensor_tensor(
                    ser_dt[:], ser_dt[:], k, exp_dt[:], ALU.add, ALU.mult), [t])
                yield
            mk = op("vector", "small", lambda e: e.tensor_scalar(exp_dt[:].bitcast(u32), exp_dt[:], 2.0 ** -6, None, ALU.is_lt), [t, ln])
            yield
            t = op("vector", "log1p", lambda e: e.copy_predicated(du[:, s2], exp_dt[:].bitcast(u32), ser_dt[:]), [mk, ln])
            yield
            t = op("vector", "delta", lambda e: e.scalar_tensor_tensor(
                delta[:, s2], delta[:, s2], 0.0, du[:, s2], ALU.max, ALU.add), [t])
            last["conv"] = last["tanh_c"] = delta_ready[c] = t
            yield
            scan_in_ready[c] = op("vector", "du", lambda e: e.tensor_tensor(du[:, s2], delta[:, s2], xc[:, s2], ALU.mult), [t])
            yield
            yield from until(lambda: c < 2 or c - 2 in z_free)
            for h in range(HALVES):
                g, free = yield from take(FRONT)
                mm = op("tensor", "in_proj", lambda e, h=h, g=g: e.matmul(
                    work_bank[g][:], w_in[:, D_INNER + h * P:D_INNER + (h + 1) * P], u_t[:, s2, :], start=True, stop=True), [free, u_made[c]])
                yield
                th = op("scalar", "tanh_z", lambda e, g=g, h=h: e.activation(silu_z[:, s2, h, :], work_bank[g][:], ACT.Tanh), [mm, prior(z_free, c - 2)])
                yield
                z = op("vector", "silu_z", lambda e, h=h, g=g: e.scalar_tensor_tensor(
                    silu_z[:, s2, h, :], silu_z[:, s2, h, :], 1.0, work_bank[g][:], ALU.add, ALU.mult), [th])
                release(g, z)
                yield
            z_made[c] = mm
            z_ready[c] = z

        inflow_ready, b_fetched, c_fetched, scanned, multiplied, summed, carried = {}, {}, {}, {}, {}, {}, {}
        decayed = {}
        units = [(c, n) for c in range(CHUNKS) for n in range(D_STATE)]
        last_y_read = {}

        def fetch(wide, name, i, row, freed):
            c, n = units[i]
            return op("sync", f"dma_{name}{i % ROW_SLOTS}", lambda e: e.dma_start(
                wide[:, i % ROW_SLOTS, :], bc_dram[c][row:row + 1, :].to_broadcast([P, CHUNK])), [bc_sent[c], freed])

        def fetch_b(i):
            if i < len(units):
                b_fetched[i] = fetch(b_wide, "b", i, units[i][1], inflow_ready.get(i - ROW_SLOTS))

        def fetch_c(i):
            if i < len(units):
                c_fetched[i] = fetch(c_wide, "c", i, D_STATE + units[i][1], multiplied.get(i - ROW_SLOTS))

        def prepare(i):
            if i >= len(units):
                return
            c, n = units[i]
            inflow_ready[i] = du_read[c] = op("gpsimd", "inflow", lambda e: e.tensor_tensor(
                inflow[:, i % 3], du[:, c % 2], b_wide[:, i % ROW_SLOTS:i % ROW_SLOTS + 1, :].to_broadcast([P, HALVES, CHUNK]), ALU.mult),
                [b_fetched[i], scan_in_ready[c], scanned.get(i - 3)])

        def decay(i, h):
            if i >= len(units):
                return
            c, n = units[i]
            decayed[(i, h)] = d_read[c] = op("scalar", "decay", lambda e: e.activation(
                decayed_by[:, i % 2, h, :], delta[:, c % 2, h, :], ACT.Exp, scale=a_neg[:, h, n:n + 1]),
                [scan_in_ready[c], a_ready, scanned.get((i - 2, h))])

        def scan(i, h):
            c, n = units[i]
            initial = 0.0 if c % (SEQ // CHUNK) == 0 else carry[:, n, h:h + 1]
            scanned[(i, h)] = scanned[i] = op("vector", "scanned", lambda e: e.tensor_tensor_scan(
                state[:, i % STATE_SLOTS, h, :], decayed_by[:, i % 2, h, :], inflow[:, i % 3, h, :], initial, ALU.mult, ALU.add),
                [decayed[(i, h)], inflow_ready[i], summed.get(i - STATE_SLOTS), carried.get(i - D_STATE)])

        def times_c(i):
            c, n = units[i]
            carried[i] = op("vector", "carried", lambda e: e.tensor_copy(carry[:, n, :], state[:, i % STATE_SLOTS, :, CHUNK - 1]), [scanned[i]])
            multiplied[i] = op("vector", "times_c", lambda e: e.tensor_tensor(
                state[:, i % STATE_SLOTS], state[:, i % STATE_SLOTS], c_wide[:, i % ROW_SLOTS:i % ROW_SLOTS + 1, :].to_broadcast([P, HALVES, CHUNK]), ALU.mult),
                [carried[i], c_fetched[i]])

        def total(i):
            c, n = units[i]
            for h in range(HALVES):
                if n == 0:
                    xc_free[c] = op("tensor", "y_skip", lambda e, h=h: e.matmul(
                        y_bank[h][:], diag_d[:, h, :], xc[:, c % 2, h, :], start=True, stop=False),
                        [xc_ready[c], diag_ready, last_y_read.get((c - 1, h))])
                summed[i] = op("tensor", "y_sum", lambda e, h=h: e.matmul(
                    y_bank[h][:], ident[:], state[:, i % STATE_SLOTS, h, :], start=False, stop=n == D_STATE - 1), [multiplied[i]])
            if n == D_STATE - 1:
                y_done[c] = summed[i]

        def take_y(c):
            s2 = c % 2
            for h in range(HALVES):
                t = op("vector", "y_gate", lambda e, h=h: e.tensor_tensor(
                    y_gated[:, h, :], silu_z[:, s2, h, :], y_bank[h][:], ALU.mult), [y_done[c], z_ready[c], last.get("y_gated")])
                last_y_read[(c, h)] = t
            z_free[c] = last["y_gate"] = t

        x_four_ready, row_sent, experts_ready, slots_loaded, combined = {}, {}, {}, {}, {}
        gate_done, expert_reg, up_done, tanh_ready, h_turned, down_done, cols_made = {}, {}, {}, {}, {}, {}, {}

        def back(c):
            sx, s2 = c % 3, c % 2
            g, free = work(SIDE)
            for s in range(SUB):
                for h in range(HALVES):
                    mm = op("tensor", "out_proj", lambda e, s=s, h=h, g=g: e.matmul(
                        work_bank[g][:, s * P:(s + 1) * P], y_gated[:, h, s * P:(s + 1) * P], w_out[:, h, :],
                        start=h == 0, stop=h == HALVES - 1), [last["y_gate"], free, back_w])
            last["y_gated"] = mm
            yield
            t = op("vector", "x_two", lambda e, g=g: e.tensor_tensor(
                x_two[:], x_one[:, sx], work_bank[g][:].rearrange("p (s d) -> p s d", s=SUB), ALU.add), [mm, x_one_ready[c]])
            x_one_free[c] = release(g, t)
            x2 = t
            xb = op("gpsimd", "x_plus_b", lambda e: e.tensor_tensor(
                x_tok[:, c], x_tok[:, c], b_ffp[:].rearrange("p (o d) -> p o d", o=1).to_broadcast([P, SUB, D_MODEL]), ALU.add), [x_one_ready[c], back_w])
            yield
            yield from norm(x_two, n_tok, 2, [t], [last.get("m_tok"), prior(row_sent, c - 1)])
            t = last[("normed", 2)]
            g, t = transposes(SIDE, n_tok, [t])
            last["n_tok"] = t
            yield
            t = op("scalar", "n_t", lambda e, g=g: e.activation(n_t[:], work_bank[g][:], ACT.Identity,
                                                              bias=norm_gb[:, 3:4], scale=norm_gb[:, 2:3]), [t, last.get("m_t")])
            release(g, t)
            g, free = work(SIDE)
            mm = op("tensor", "ff_gate", lambda e, g=g: e.matmul(work_bank[g][:], w_ffg[:, 0:P], n_t[:], start=True, stop=True),
                    [t, free, back_ready[0]])
            yield
            th = op("scalar", "tanh_g", lambda e, g=g: e.activation(tanh_g[:], work_bank[g][:], ACT.Tanh, bias=b_ffg[:, 0:1]), [mm, last.get("gate_h")])
            t = op("scalar", "gate_h", lambda e, g=g: e.activation(gate_h[:], work_bank[g][:], ACT.Identity, bias=b_ffg[:, 0:1]), [mm, last.get("ff_h")])
            release(g, t)
            g, free = work(SIDE)
            mm = op("tensor", "ff_val", lambda e, g=g: e.matmul(work_bank[g][:], w_ffg[:, P:], n_t[:], start=True, stop=True), [free])
            last["n_t"] = mm
            yield
            t = op("vector", "silu_g", lambda e: e.scalar_tensor_tensor(gate_h[:], tanh_g[:], 1.0, gate_h[:], ALU.add, ALU.mult), [t, th])
            t = op("vector", "ff_h", lambda e, g=g: e.scalar_tensor_tensor(
                ff_h[:], work_bank[g][:], b_ffg[:, 1:2], gate_h[:], ALU.add, ALU.mult), [t, mm, last.get("ff_h")])
            last["gate_h"] = release(g, t)
            g, free = work(SIDE)
            for s in range(SUB):
                mm = op("tensor", "ff_out", lambda e, s=s, g=g: e.matmul(
                    work_bank[g][:, s * P:(s + 1) * P], ff_h[:, s * P:(s + 1) * P], w_ffp[:], start=True, stop=True), [t, free])
            last["ff_h"] = mm
            yield
            t = op("vector", "x_three", lambda e, g=g: e.tensor_tensor(
                x_two[:], x_two[:], work_bank[g][:].rearrange("p (s d) -> p s d", s=SUB), ALU.add), [mm])
            release(g, t)
            t = x_four_ready[c] = op("vector", "x_four", lambda e: e.tensor_tensor(x_tok[:, c], x_two[:], x_tok[:, c], ALU.add), [t, xb])
            yield
            yield from norm(x_tok[:, c], m_tok, 3, [t], [last.get("n_tok")])
            t = last[("normed", 3)]
            group = next(k for k, cs in enumerate(GROUPS) if c in cs)
            at = c - GROUPS[group][0]
            row_sent[c] = op("sync", f"dma_rows{s2}", lambda e: e.dma_start(
                row_dram[group][at * CHUNK:(at + 1) * CHUNK].rearrange("(s p) d -> p s d", p=P), m_tok[:]), [t])
            g, t = transposes(SIDE, m_tok, [t])
            last["m_tok"] = t
            yield
            t = op("scalar", "m_t", lambda e, g=g: e.activation(m_t[:], work_bank[g][:], ACT.Copy), [t, last["n_t"]])
            release(g, t)
            yield
            g, free = work(SIDE)
            for s in range(SUB):
                mm = op("tensor", "route", lambda e, s=s, g=g: e.matmul(
                    work_bank[g][:, s * EXPERTS:(s + 1) * EXPERTS], m_t[:, s * P:(s + 1) * P], w_route[:], start=True, stop=True), [t, free])
            last["m_t"] = mm
            yield
            t = op("vector", "logits", lambda e, g=g: e.tensor_tensor(
                logits[:], work_bank[g][:, :SUB * EXPERTS].rearrange("p (s e) -> p s e", s=SUB),
                b_route[:].rearrange("p (o e) -> p o e", o=1).to_broadcast([P, SUB, EXPERTS]), ALU.add), [mm, last.get("logits")])
            release(g, t)
            for s in range(SUB):
                mx = op("vector", "top", lambda e, s=s: e.max(top8[:, s, :], logits[:, s, :]), [t, last.get("top8")])
            for s in range(SUB):
                ix = op("vector", "top", lambda e, s=s: e.max_index(top_i[:, s, :], top8[:, s, :], logits[:, s, :]), [mx, last.get("logits")])
            gap = op("vector", "gap", lambda e: e.tensor_tensor(top_w[:, 0, :], top8[:, :, 1], top8[:, :, 0], ALU.subtract), [ix, last.get("top_w")])
            last["top8"] = gap
            t = last["logits"] = op("vector", "top", lambda e: e.tensor_copy(top_if[:], top_i[:]), [ix, last.get("choice")])
            ex = op("scalar", "route_exp", lambda e: e.activation(top_w[:, 0, :], top_w[:, 0, :], ACT.Exp), [gap])
            yield
            tiles = slice(c * SUB, (c + 1) * SUB)
            for k in range(TOPK):
                t2 = op("vector", "choice", lambda e, k=k: e.tensor_tensor(
                    choice[:, k, tiles, :], iota8[:].rearrange("p (o e) -> p o e", o=1).to_broadcast([P, SUB, EXPERTS]),
                    top_if[:, :, k:k + 1].to_broadcast([P, SUB, EXPERTS]), ALU.is_equal), [t])
            last["choice"] = t2
            chosen = op("vector", "both", lambda e: e.tensor_tensor(both[:], choice[:, 0, tiles, :], choice[:, 1, tiles, :], ALU.add), [t2, last.get("both")])
            t = op("vector", "weights", lambda e: e.tensor_scalar(top_w[:, 1, :], top_w[:, 0, :], 1.0, None, ALU.add), [ex])
            t = op("vector", "weights", lambda e: e.reciprocal(choice_w[:, 0, tiles], top_w[:, 1, :]), [t])
            t = last["top_w"] = op("vector", "weights", lambda e: e.tensor_tensor(choice_w[:, 1, tiles], top_w[:, 0, :], choice_w[:, 0, tiles], ALU.mult), [t])
            yield
            g, free = work(SIDE)
            op("tensor", "rank", lambda e, g=g: e.matmul(work_bank[g][:, 0:SUB * EXPERTS], before[:], both[:].rearrange("p s e -> p (s e)"),
                                                       start=True, stop=True), [chosen, free])
            mm = last["both"] = op("tensor", "rank", lambda e, g=g: e.matmul(
                work_bank[g][:, SUB * EXPERTS:2 * SUB * EXPERTS], ones[:], both[:].rearrange("p s e -> p (s e)"), start=True, stop=True), [ones_made])
            yield
            t = op("vector", "tile_sum", lambda e, g=g: e.tensor_copy(
                tile_sum[:].rearrange("p k s e -> p (k s e)"), work_bank[g][:, 0:2 * SUB * EXPERTS]), [mm, last.get("tile_sum")])
            release(g, t)
            if c == GROUPS[group][0]:
                t = op("vector", "count", lambda e: e.memset(count[:, 0, :], 0.0), [t, last.get("count")])
            for s in range(SUB):
                op("vector", "count", lambda e, s=s: e.tensor_tensor(
                    rank[:, c * SUB + s, :], tile_sum[:, 0, s, :], count[:, s % 2, :], ALU.add), [t, last.get("count")])
                t = last["count"] = op("vector", "count", lambda e, s=s: e.tensor_tensor(
                    count[:, 1 - s % 2, :], tile_sum[:, 1, s, :], count[:, s % 2, :], ALU.add), [t])
            last["tile_sum"] = t
            yield
            if c == GROUPS[group][-1]:
                yield from sort_pairs(group, t)

        def sort_pairs(k, counted):
            chunks, n_tiles = GROUPS[k], TILES[k]
            first, n_tok = chunks[0] * SUB, len(chunks) * SUB
            mine = slice(first, first + n_tok)
            t = op("vector", "sort", lambda e: e.tensor_scalar(tiles_i[:], count[:, 0, :], float(P - 1), None, ALU.add), [counted, last.get("sort")])
            t = op("vector", "sort", lambda e: e.tensor_single_scalar(tiles_i[:], tiles_i[:], 7, ALU.arith_shift_right), [t])
            t = op("vector", "sort", lambda e: e.tensor_copy(tiles_f[:], tiles_i[:]), [t])
            t = op("vector", "sort", lambda e: e.tensor_tensor_scan(tiles_end[:], ones[:, 0:EXPERTS], tiles_f[:], 0.0, ALU.mult, ALU.add), [t, ones_made])
            t = op("vector", "sort", lambda e: e.tensor_tensor(start[:], tiles_end[:], tiles_f[:], ALU.subtract), [t])
            t = op("vector", "sort", lambda e: e.tensor_scalar(start[:], start[:], float(P), None, ALU.mult), [t])
            t = op("vector", "sort", lambda e: e.tensor_tensor(
                passed[:, :n_tiles, :], iota_tile[:, :n_tiles].rearrange("p (j o) -> p j o", o=1).to_broadcast([P, n_tiles, EXPERTS]),
                tiles_end[:].rearrange("p (o e) -> p o e", o=1).to_broadcast([P, n_tiles, EXPERTS]), ALU.is_ge), [t])
            t = op("vector", "sort", lambda e: e.tensor_reduce(expert_f[:, :n_tiles], passed[:, :n_tiles, :], AX.X, ALU.add), [t])
            t = op("vector", "sort", lambda e: e.tensor_scalar(expert_i[:, k, :n_tiles], expert_f[:, :n_tiles], float(EXPERTS - 1), None, ALU.min), [t])
            experts_ready[k] = t
            yield
            t = op("vector", "sort", lambda e: e.tensor_tensor(
                rank[:, mine, :], rank[:, mine, :], start[:].rearrange("p (o e) -> p o e", o=1).to_broadcast([P, n_tok, EXPERTS]), ALU.add), [t])
            for q in range(TOPK):
                t2 = op("vector", "sort", lambda e, q=q: e.tensor_tensor(picked[:, q, :n_tok, :], rank[:, mine, :], choice[:, q, mine, :], ALU.mult), [t])
            t = op("vector", "sort", lambda e: e.tensor_reduce(place_f[:, :, :n_tok], picked[:, :, :n_tok, :], AX.X, ALU.add), [t2])
            t = op("vector", "sort", lambda e: e.tensor_copy(place[:, :, mine], place_f[:, :, :n_tok]), [t])
            yield
            t = op("vector", "sort", lambda e: e.tensor_single_scalar(place_hi[:, :, :n_tok], place[:, :, mine].bitcast(i32), 7, ALU.arith_shift_right), [t])
            t = op("vector", "sort", lambda e: e.tensor_copy(place_hf[:, :, :n_tok], place_hi[:, :, :n_tok]), [t, last.get("hot")])
            t = last["sort"] = op("vector", "sort", lambda e: e.scalar_tensor_tensor(
                place_lf[:, :, :n_tok], place_hf[:, :, :n_tok], -float(P), place_f[:, :, :n_tok], ALU.mult, ALU.add), [t])
            yield
            g, free = work(SIDE)
            for at in range(0, n_tok, SUB):
                for q in range(TOPK):
                    lo = op("vector", "hot", lambda e, at=at, q=q: e.tensor_tensor(
                        hot_lo[:], iota_p[:].rearrange("p (o m) -> p o m", o=1).to_broadcast([P, SUB, P]),
                        place_lf[:, q, at:at + SUB].rearrange("p (s o) -> p s o", o=1).to_broadcast([P, SUB, P]), ALU.is_equal), [t, last.get("hot")])
                    hi = op("vector", "hot", lambda e, at=at, q=q: e.tensor_tensor(
                        hot_hi[:, :, :n_tiles], iota_tile[:, :n_tiles].rearrange("p (o m) -> p o m", o=1).to_broadcast([P, SUB, n_tiles]),
                        place_hf[:, q, at:at + SUB].rearrange("p (s o) -> p s o", o=1).to_broadcast([P, SUB, n_tiles]), ALU.is_equal))
                    hi = op("vector", "hot", lambda e, at=at: e.tensor_tensor(
                        hot_hi[:, :, :n_tiles], hot_hi[:, :, :n_tiles],
                        token_id[:, at:at + SUB].rearrange("p (s o) -> p s o", o=1).to_broadcast([P, SUB, n_tiles]), ALU.mult), [hi])
                    for s in range(SUB):
                        last["hot"] = op("tensor", "slot_sum", lambda e, s=s, g=g, at=at, q=q: e.matmul(
                            work_bank[g][:, :n_tiles], hot_lo[:, s, :], hot_hi[:, s, :n_tiles],
                            start=at + q + s == 0, stop=at + q + s == n_tok + TOPK - 2), [hi, free])
                    yield
            slots_loaded[k] = release(g, op("vector", "slot_token", lambda e, g=g: e.tensor_copy(
                slot_token[:, k, :n_tiles], work_bank[g][:, :n_tiles]), [last["hot"]]))
            yield

        gathered, cols_ready, h_ready, g_free, y_sent = {}, {}, {}, {}, {}
        jobs = [(k, j) for k, n in enumerate(TILES) for j in range(n)]

        def gather(m):
            if m >= len(jobs) or m in gathered:
                return
            k, j = jobs[m]
            if k not in slots_loaded:
                return
            gathered[m] = op("gpsimd", f"dma_gather{m % 3}", lambda e: e.indirect_dma_start(
                x_rows[:, m % 3, :], None, row_dram[k], bass.IndirectOffsetOnAxis(slot_token[:, k, j:j + 1], 0)),
                [slots_loaded[k], row_sent[GROUPS[k][-1]], row_sent[GROUPS[k][-1] - 1], cols_ready.get(m - 3)])

        def turn_rows(m, banks):
            if m not in gathered or m in cols_ready:
                return None
            return op("tensor", "x_turned", lambda e: e.transpose(banks[0][:, NF * P:], x_rows[:, m % 3, :], ident[:]), [gathered[m], g_free.get(id(banks[0]))])

        def copy_rows(m, banks, turned):
            if turned:
                cols_ready[m] = g_free[id(banks[0])] = op("scalar", "x_cols", lambda e: e.activation(
                    x_cols[:, m % 2, :], banks[0][:, NF * P:], ACT.Copy), [turned, up_done.get(m - 2)])

        def tile_up(m, banks):
            k, j = jobs[m]

            def read_expert(e, m, j):
                expert_reg[m] = e.value_load(expert_i[0:1, k, j:j + 1], min_val=0, max_val=EXPERTS - 1)

            def gate(e):
                if m not in expert_reg:
                    read_expert(e, m, j)
                return e.matmul(banks[0][:, 0:FF], x_cols[:, m % 2, :], w_gate[:, bass.ds(expert_reg[m], 1), :].rearrange("p o f -> p (o f)"), start=True, stop=True)

            def up(e):
                done = e.matmul(banks[1][:, 0:FF], x_cols[:, m % 2, :], w_up[:, bass.ds(expert_reg[m], 1), :].rearrange("p o f -> p (o f)"), start=True, stop=True)
                if j + 1 < TILES[k]:
                    read_expert(e, m + 1, j + 1)
                return done

            gate_done[m] = op("tensor", "moe_gate", gate, [cols_ready[m], experts_ready[k], g_free.get(id(banks[0])), back_ready[0]])
            up_done[m] = op("tensor", "moe_up", up, [g_free.get(id(banks[1]))])

        def tile_tanh(m, banks):
            tanh_ready[m] = op("scalar", "tanh_m", lambda e: e.activation(h_rows[:, m % 2, :], banks[0][:, 0:FF], ACT.Tanh), [gate_done[m], h_turned.get(m - 2)])

        def tile_h(m, banks):
            t = op("vector", "silu_m", lambda e: e.scalar_tensor_tensor(
                silu_m[:], h_rows[:, m % 2, :], 1.0, banks[0][:, 0:FF], ALU.add, ALU.mult), [tanh_ready[m], h_ready.get(m - 1)])
            h_ready[m] = g_free[id(banks[0])] = op("vector", "moe_h", lambda e: e.tensor_tensor(
                h_rows[:, m % 2, :], silu_m[:], banks[1][:, 0:FF], ALU.mult), [t, up_done[m]])
            g_free[id(banks[1])] = h_ready[m]

        def tile_turn(m, banks, follow=None):
            for q, (f, n) in enumerate(F_TILES):
                mm = op("tensor", "h_turned", lambda e, q=q, f=f, n=n: e.transpose(
                    banks[0][:n, q * P:(q + 1) * P], h_rows[:, m % 2, f:f + n], ident[:]), [h_ready[m], g_free[id(banks[0])]])
            h_turned[m] = mm
            turned = turn_rows(follow, banks) if follow is not None else None
            f, n = F_TILES[-1]
            full = NF - 1
            op("scalar", "h_cols", lambda e: e.activation(
                h_cols[:, m % 2, 0:full, :], banks[0][:, 0:full * P].rearrange("p (q t) -> p q t", q=full), ACT.Copy), [turned or mm, down_done.get(m - 2)])
            cols_made[m] = g_free[id(banks[0])] = op("scalar", "h_cols", lambda e: e.activation(
                h_cols[:n, m % 2, full, :], banks[0][:n, full * P:NF * P], ACT.Copy))
            copy_rows(follow, banks, turned)

        def tile_down(m, banks):
            t = cols_made[m]
            for q, (f, n) in enumerate(F_TILES):
                mm = op("tensor", "moe_down", lambda e, q=q, n=n: e.matmul(
                    banks[1][:, 0:D_MODEL], h_cols[:n, m % 2, q, :], w_down[:n, bass.ds(expert_reg[m], 1), q, :].rearrange("p o d -> p (o d)"),
                    start=q == 0, stop=q == NF - 1), [t, g_free[id(banks[1])]])
            down_done[m] = mm

        def tile_out(m, banks):
            k, j = jobs[m]
            t = g_free[id(banks[1])] = op("scalar", "y_rows", lambda e: e.activation(y_rows[:, m % 2, :], banks[1][:, 0:D_MODEL], ACT.Copy), [down_done[m], y_sent.get(m - 2)])
            y_sent[m] = op("sync", f"dma_y{m % 2}", lambda e: e.dma_start(y_dram[k][j * P:(j + 1) * P, :], y_rows[:, m % 2, :]), [t])

        def combine(k):
            ends = [y_sent[m] for m in range(len(jobs)) if jobs[m][0] == k][-2:]
            for c in GROUPS[k]:
                for s in range(SUB):
                    tile = c * SUB + s
                    got = []
                    for q in range(TOPK):
                        got.append(op("gpsimd", f"dma_pair{tile % 2}", lambda e, q=q, tile=tile: e.indirect_dma_start(
                            y_pair[:, tile % 2, q, :], None, y_dram[k], bass.IndirectOffsetOnAxis(place[:, q, tile:tile + 1], 0)),
                            ends + [combined.get(tile - 2)]))
                    yield
                    for q in range(TOPK):
                        t = op("vector", "combined", lambda e, q=q, s=s, c=c, tile=tile: e.scalar_tensor_tensor(
                            x_tok[:, c, s, :], y_pair[:, tile % 2, q, :], choice_w[:, q, tile:tile + 1], x_tok[:, c, s, :], ALU.mult, ALU.add),
                            [got[-1], x_four_ready[c], combined.get(tile) if q else None])
                        combined[tile] = t
                out_sent[c] = op("sync", "dma_out", lambda e, c=c: e.dma_start(out_dram[c], x_tok[:, c]), [t])
                yield

        def step(gens, n=1):
            for _ in range(n):
                while gens and next(gens[0], "over") == "over":
                    gens.pop(0)

        fronts_a = [front_a(c) for c in range(CHUNKS)]
        fronts_b = [front_b(c) for c in range(CHUNKS)]
        first = [fronts_a.pop(0)]
        while 0 not in u_made:
            step(first)
        for _ in range(HEAD_STEPS):
            step(first)
            step(fronts_a)
        halve_back()
        step(first, 99)
        while 0 not in scan_in_ready:
            step(fronts_b)
        for i in range(ROW_SLOTS):
            fetch_b(i)
        for i in range(2):
            fetch_c(i)
            prepare(i)
        fetch_b(ROW_SLOTS)
        for h in range(HALVES):
            decay(0, h)
        for h in range(HALVES):
            decay(1, h)
        sides, combining = [], []
        m, waiting = 0, False

        def after_tile(m):
            k, j = jobs[m]
            if j == TILES[k] - 1:
                combining.append(combine(k))

        for i in range(len(units)):
            c, n = units[i]
            now[0] = i
            while c + 1 < CHUNKS and (n == D_STATE - 5 and c + 1 not in bc_sent or n == D_STATE - 3 and c + 1 not in scan_in_ready):
                step(fronts_a)
                step(fronts_b)
            fetch_b(i + 4)
            fetch_c(i + 2)
            prepare(i + 2)
            moving = m < len(jobs) and m in cols_ready
            last_tile = m - 1
            if not moving and m < len(jobs) and jobs[m][0] in slots_loaded:
                gather(m), gather(m + 1), gather(m + 2)
                copy_rows(m, expert_banks[m % 2], turn_rows(m, expert_banks[m % 2]))
            if waiting:
                tile_turn(m - 1, expert_banks[(m - 1) % 2], follow=m + 1 if moving else None)
            elif moving:
                copy_rows(m + 1, expert_banks[(m + 1) % 2], turn_rows(m + 1, expert_banks[(m + 1) % 2]))
            if moving:
                tile_up(m, expert_banks[m % 2])
                tile_tanh(m, expert_banks[m % 2])
            scan(i, 0)
            decay(i + 2, 0)
            scan(i, 1)
            decay(i + 2, 1)
            if i:
                total(i - 1)
            step(fronts_a)
            if moving:
                tile_h(m, expert_banks[m % 2])
            if waiting:
                tile_down(m - 1, expert_banks[(m - 1) % 2])
            if n == 0 and c:
                take_y(c - 1)
                sides.append(back(c - 1))
            step(sides)
            step(fronts_b)
            times_c(i)
            if moving:
                gather(m + 3)
                m += 1
            step(fronts_a)
            if c == 0 or c + 1 in scan_in_ready:
                step(fronts_b)
            step(sides)
            if waiting:
                tile_out(last_tile, expert_banks[last_tile % 2])
                after_tile(last_tile)
            waiting = moving
            if i % 2:
                step(combining)
        total(len(units) - 1)
        take_y(CHUNKS - 1)
        sides.append(back(CHUNKS - 1))
        pairs = {m % 3: expert_banks[m % 2], (m + 1) % 3: expert_banks[(m + 1) % 2], (m + 2) % 3: y_bank}
        for h, b in enumerate(y_bank):
            g_free[id(b)] = last_y_read[(CHUNKS - 1, h)]
        if waiting:
            tile_turn(m - 1, expert_banks[(m - 1) % 2])
            tile_down(m - 1, expert_banks[(m - 1) % 2])
            tile_out(m - 1, expert_banks[(m - 1) % 2])
            after_tile(m - 1)
        step(sides, 2)
        rest = list(range(m, len(jobs)))
        if jobs[m][0] not in slots_loaded:
            step(sides, 999)
        for q in rest[:3]:
            gather(q)

        def turn_next(q):
            copy_rows(q, pairs[q % 3], turn_rows(q, pairs[q % 3]))

        if rest[0] not in cols_ready:
            turn_next(rest[0])
        for q in rest + [len(jobs), len(jobs) + 1]:
            if q + 1 < len(jobs):
                turn_next(q + 1)
            if q < len(jobs):
                tile_up(q, pairs[q % 3])
                tile_tanh(q, pairs[q % 3])
            step(sides, 1)
            if rest[0] < q <= len(jobs):
                tile_turn(q - 1, pairs[(q - 1) % 3])
            if q < len(jobs):
                tile_h(q, pairs[q % 3])
            if q >= rest[0] + 2:
                tile_down(q - 2, pairs[(q - 2) % 3])
                tile_out(q - 2, pairs[(q - 2) % 3])
                after_tile(q - 2)
            step(sides, 1)
            if q + 1 < len(jobs) and jobs[q + 1][0] not in slots_loaded:
                step(sides, 999)
            for follower in range(q + 1, q + 4):
                gather(follower)
            step(combining)
        step(combining, 999)
        pr.wait("sync", [("dma_out", 16 * CHUNKS)] + [y_sent[q] for q in range(len(jobs) - 2, len(jobs))] + [row_sent[CHUNKS - 1], row_sent[CHUNKS - 2], bc_sent[CHUNKS - 1]])

        block = ctx.enter_context(nc.Block())

        @block.sync
        def _(eng):
            pr.play("sync", eng)

        @block.gpsimd
        def _(eng):
            pr.play("gpsimd", eng)

        @block.scalar
        def _(eng):
            pr.play("scalar", eng)

        @block.vector
        def _(eng):
            pr.play("vector", eng)

        @block.tensor
        def _(eng):
            pr.play("tensor", eng)


def shape_constants():
    ident = np.eye(P, dtype=np.float32)
    iota8 = np.tile(np.arange(EXPERTS, dtype=np.float32), (P, 1))
    iota_tile = np.tile(np.arange(max(TILES), dtype=np.float32), (P, 1))
    before = np.triu(np.ones((P, P), np.float32), 1)
    token_id = np.arange(TOKENS, dtype=np.float32).reshape(-1, P).T
    return {"ident": ident, "iota8": iota8,
            "iota_tile": iota_tile, "iota_p": np.tile(np.arange(P, dtype=np.float32), (P, 1)), "before": before, "token_id": token_id}


def columns(vector):
    return vector.reshape(-1, P).T


def kernel(**inputs):
    import concourse.bacc as bacc
    from concourse.bass_utils import run_bass_kernel_spmd as run

    a = {k.replace("L0_attn_", "").replace("L0_ffn_", ""): np.asarray(v) for k, v in inputs.items()}
    xproj = a["x_proj_w"]
    dt_rows, bc_rows = xproj[:DT_RANK], xproj[DT_RANK:]
    arrays = {
        "x": a["x"], **shape_constants(),
        "in_wT": a["in_proj_w"].T, "norm_gb": np.stack([a["n1_g"], a["n1_b"], a["n2_g"], a["n2_b"]], 1),
        "conv_w": a["conv_w"], "conv_b": columns(a["conv_b"]),
        "xproj_wT": np.concatenate([bc_rows, dt_rows], 0).T,
        "dt_wT": a["dt_w"].T, "dt_b": columns(a["dt_b"]), "A_log": a["A_log"], "D": columns(a["D"]), "out_wT": a["out_w"].T,
        "ffg_wT": a["ffg_w"].T, "ffg_b": columns(a["ffg_b"]), "ffp_wT": a["ffp_w"].T, "ffp_b": a["ffp_b"],
        "Ws": a["Ws"], "bs": a["bs"], "Wg": a["Wg"], "Wu": a["Wu"], "Wd": a["Wd"],
    }
    nc = bacc.Bacc("TRN2", target_bir_lowering=False, num_devices=1)
    feeds, T = {}, {}
    for name, array in arrays.items():
        array = np.ascontiguousarray(array)
        feeds[f"in_{name}"] = array
        T[name] = nc.dram_tensor(f"in_{name}", array.shape, mybir.dt.from_np(array.dtype), kind="ExternalInput").ap()
    out = nc.dram_tensor("out_0", (BATCH, SEQ, D_MODEL), mybir.dt.float32, kind="ExternalOutput").ap()
    mamba_moe_block(nc, T, out)
    result = run(nc, [feeds], core_ids=[0])
    return result.results[0]["out_0"]
```
